# Optimizing a Trainium2 kernel written in Bass

```python
import numpy as np
import jax
import jax.numpy as jnp

def _softmax(x, axis=-1):
    return jax.nn.softmax(x, axis=axis)

def _gelu(x):
    return jax.nn.gelu(x, approximate=True)

def _silu(x):
    return jax.nn.silu(x)

def _sigmoid(x):
    return jax.nn.sigmoid(x)

def _layernorm(x, axis=-1, eps=1e-05):
    m = jnp.mean(x, axis=axis, keepdims=True)
    v = jnp.var(x, axis=axis, keepdims=True)
    return (x - m) / jnp.sqrt(v + eps)

def _scatter_add(tgt, idx, src, axis=0):
    return tgt.at[idx].add(src)

def _segment_sum(src, seg, n):
    return jax.ops.segment_sum(src, seg, n)
kernel_name = 'mk_sandwich_d1_jaxref_r2_f86633'

def setup_inputs(seed: int=0):
    np.random.seed(seed)
    _w = jnp.asarray

    def _L0_attn_setup():
        import jax, jax.numpy as jnp
        import numpy as np
        DIM = 512
        HEADS = 16
        HEAD_DIM = DIM // HEADS
        WINDOW = 256
        NEG = -1000000000.0

        def _sliding_window_attn(x, Wq, bq, Wk, bk, Wv, bv, Wo, bo):
            B, S, D = x.shape
            H, hd, W = (HEADS, HEAD_DIM, WINDOW)
            nb = S // W

            def proj(Wp, bp):
                y = x @ Wp.T + bp
                return y.reshape(B, S, H, hd).transpose(0, 2, 1, 3)
            q = proj(Wq, bq)
            k = proj(Wk, bk)
            v = proj(Wv, bv)
            scale = hd ** (-0.5)
            qb = q.reshape(B, H, nb, W, hd)

            def window_kv(t):
                pad = jnp.concatenate([jnp.zeros((B, H, W, hd), t.dtype), t], axis=2)
                prev = pad[:, :, :S].reshape(B, H, nb, W, hd)
                cur = t.reshape(B, H, nb, W, hd)
                return jnp.concatenate([prev, cur], axis=3)
            kw = window_kv(k)
            vw = window_kv(v)
            scores = jnp.einsum('bhnqd,bhnkd->bhnqk', qb, kw) * scale
            t = jnp.arange(2 * W)
            s_ = jnp.arange(W)[:, None]
            n = jnp.arange(nb)[:, None, None]
            valid = (t <= s_ + W) & (t >= s_ + 1) & (n * W - W + t >= 0)
            scores = jnp.where(valid, scores, NEG)
            attn = jax.nn.softmax(scores, axis=-1)
            out = jnp.einsum('bhnqk,bhnkd->bhnqd', attn, vw)
            out = out.reshape(B, H, S, hd).transpose(0, 2, 1, 3).reshape(B, S, D)
            return out @ Wo.T + bo
        key = jax.random.key(seed)
        ks = jax.random.split(key, 9)
        s = 1.0 / np.sqrt(DIM)
        inp = {'x': jax.random.normal(ks[0], (2, 2048, DIM), dtype=jnp.float32)}
        for i, name in enumerate(['q', 'k', 'v', 'o']):
            inp[f'W{name}'] = jax.random.uniform(ks[1 + 2 * i], (DIM, DIM), jnp.float32, -s, s)
            inp[f'b{name}'] = jax.random.uniform(ks[2 + 2 * i], (DIM,), jnp.float32, -s, s)
        return inp
    _L0_attn_in = _L0_attn_setup()

    def _L0_ffn_setup():
        import jax, jax.numpy as jnp
        import numpy as np

        def _bitlinear(x, w_latent):
            scale = jax.lax.stop_gradient(jnp.clip(jnp.mean(jnp.abs(w_latent), axis=1, keepdims=True), 1e-05, None))
            tern = jnp.clip(jnp.round(w_latent / scale), -1.0, 1.0)
            w = w_latent + jax.lax.stop_gradient(tern - w_latent)
            return x @ (w * scale).T
        key = jax.random.key(seed)
        ks = jax.random.split(key, 6)
        dim, hidden, rank = (512, 2048, 16)
        B, S = (4, 2048)
        x = jax.random.normal(ks[0], (B, S, dim), dtype=jnp.float32)
        w_fc = 0.02 * jax.random.normal(ks[1], (hidden, dim), dtype=jnp.float32)
        w_proj = 0.02 * jax.random.normal(ks[2], (dim, hidden), dtype=jnp.float32)
        u = 0.02 * jax.random.normal(ks[3], (hidden, rank), dtype=jnp.float32)
        v = 0.02 * jax.random.normal(ks[4], (rank, dim), dtype=jnp.float32)
        fast_b = jax.random.normal(ks[5], (rank, rank), dtype=jnp.float32)
        gate = jnp.float32(0.05)
        return {'x': x, 'fast_b': fast_b, 'w_fc': w_fc, 'w_proj': w_proj, 'u': u, 'v': v, 'gate': gate}
    _L0_ffn_in = _L0_ffn_setup()
    _d = {'L0_attn_x': _L0_attn_in['x'], 'L0_attn_Wq': _L0_attn_in['Wq'], 'L0_attn_bq': _L0_attn_in['bq'], 'L0_attn_Wk': _L0_attn_in['Wk'], 'L0_attn_bk': _L0_attn_in['bk'], 'L0_attn_Wv': _L0_attn_in['Wv'], 'L0_attn_bv': _L0_attn_in['bv'], 'L0_attn_Wo': _L0_attn_in['Wo'], 'L0_attn_bo': _L0_attn_in['bo'], 'L0_ffn_fast_b': _L0_ffn_in['fast_b'], 'L0_ffn_w_fc': _L0_ffn_in['w_fc'], 'L0_ffn_w_proj': _L0_ffn_in['w_proj'], 'L0_ffn_u': _L0_ffn_in['u'], 'L0_ffn_v': _L0_ffn_in['v'], 'L0_ffn_gate': _L0_ffn_in['gate']}
    _x0 = _d['L0_attn_x']
    _d['L0_attn_x'] = jax.random.normal(jax.random.fold_in(jax.random.key(seed), 1), (8, 1024, 512), dtype=_x0.dtype)
    del _x0
    return _d

def reference(L0_attn_x, L0_attn_Wq, L0_attn_bq, L0_attn_Wk, L0_attn_bk, L0_attn_Wv, L0_attn_bv, L0_attn_Wo, L0_attn_bo, L0_ffn_fast_b, L0_ffn_w_fc, L0_ffn_w_proj, L0_ffn_u, L0_ffn_v, L0_ffn_gate):

    def _L0_attn_ref(x, Wq, bq, Wk, bk, Wv, bv, Wo, bo):
        import jax, jax.numpy as jnp
        import numpy as np
        DIM = 512
        HEADS = 16
        HEAD_DIM = DIM // HEADS
        WINDOW = 256
        NEG = -1000000000.0

        def _sliding_window_attn(x, Wq, bq, Wk, bk, Wv, bv, Wo, bo):
            B, S, D = x.shape
            H, hd, W = (HEADS, HEAD_DIM, WINDOW)
            nb = S // W

            def proj(Wp, bp):
                y = x @ Wp.T + bp
                return y.reshape(B, S, H, hd).transpose(0, 2, 1, 3)
            q = proj(Wq, bq)
            k = proj(Wk, bk)
            v = proj(Wv, bv)
            scale = hd ** (-0.5)
            qb = q.reshape(B, H, nb, W, hd)

            def window_kv(t):
                pad = jnp.concatenate([jnp.zeros((B, H, W, hd), t.dtype), t], axis=2)
                prev = pad[:, :, :S].reshape(B, H, nb, W, hd)
                cur = t.reshape(B, H, nb, W, hd)
                return jnp.concatenate([prev, cur], axis=3)
            kw = window_kv(k)
            vw = window_kv(v)
            scores = jnp.einsum('bhnqd,bhnkd->bhnqk', qb, kw) * scale
            t = jnp.arange(2 * W)
            s_ = jnp.arange(W)[:, None]
            n = jnp.arange(nb)[:, None, None]
            valid = (t <= s_ + W) & (t >= s_ + 1) & (n * W - W + t >= 0)
            scores = jnp.where(valid, scores, NEG)
            attn = jax.nn.softmax(scores, axis=-1)
            out = jnp.einsum('bhnqk,bhnkd->bhnqd', attn, vw)
            out = out.reshape(B, H, S, hd).transpose(0, 2, 1, 3).reshape(B, S, D)
            return out @ Wo.T + bo
        return _sliding_window_attn(x, Wq, bq, Wk, bk, Wv, bv, Wo, bo)

    def _L0_ffn_ref(x, fast_b, w_fc, w_proj, u, v, gate):
        import jax, jax.numpy as jnp
        import numpy as np

        def _bitlinear(x, w_latent):
            scale = jax.lax.stop_gradient(jnp.clip(jnp.mean(jnp.abs(w_latent), axis=1, keepdims=True), 1e-05, None))
            tern = jnp.clip(jnp.round(w_latent / scale), -1.0, 1.0)
            w = w_latent + jax.lax.stop_gradient(tern - w_latent)
            return x @ (w * scale).T
        h = _bitlinear(x, w_fc) + gate * (x @ v.T @ fast_b.T @ u.T)
        r = jnp.maximum(h, 0.0)
        return _bitlinear(r * r, w_proj)
    x = L0_attn_x
    x = x + _layernorm(_L0_attn_ref(_layernorm(x, axis=-1), L0_attn_Wq, L0_attn_bq, L0_attn_Wk, L0_attn_bk, L0_attn_Wv, L0_attn_bv, L0_attn_Wo, L0_attn_bo), axis=-1)
    x = x + _layernorm(_L0_ffn_ref(_layernorm(x, axis=-1), L0_ffn_fast_b, L0_ffn_w_fc, L0_ffn_w_proj, L0_ffn_u, L0_ffn_v, L0_ffn_gate), axis=-1)
    return x

_drawn_inputs = setup_inputs


def setup_inputs(seed=0):
    import zlib

    import numpy as np

    out = dict(_drawn_inputs(seed))
    spreads = {}
    factors = {'L0_attn_bq': 7.414,
     'L0_attn_bk': 8.0,
     'L0_ffn_fast_b': 3.788,
     'L0_ffn_u': 3.802,
     'L0_ffn_v': 3.367}
    for name, (base, spread) in spreads.items():
        noise = np.random.default_rng([zlib.crc32(name.encode()), seed]).standard_normal(out[name].shape)
        drawn = base * np.exp(spread * noise) if base else spread * noise
        out[name] = jnp.asarray(drawn.astype(out[name].dtype))
    for name, factor in factors.items():
        out[name] = (out[name] * factor).astype(out[name].dtype)
    return out
```

```python
from contextlib import ExitStack

import concourse.bass as bass
from concourse import mybir

P = 128
BATCH, SEQ, D = 8, 1024, 512
HEADS, HD = 16, 32
HIDDEN, RANK = 2048, 16
WINDOW = 256
STEP = 256
TILES = STEP // P
PER_SEQ = SEQ // STEP
NSTEP = BATCH * PER_SEQ
KD = D // P
KH = HIDDEN // P
GROUP = P // HD
NGROUP = HEADS // GROUP
SLOTS = NGROUP * TILES * GROUP
NKC = WINDOW // P + 1
WIN = NKC * P
RING = 2 * STEP
ST = 3 * HD
LR = 6 * RANK
EPS = 1e-5
XS = 2.0 ** 11
NEG = -1e38

F32, F16, BF16, U32 = mybir.dt.float32, mybir.dt.float16, mybir.dt.bfloat16, mybir.dt.uint32
ALU, ACT, AX = mybir.AluOpType, mybir.ActivationFunctionType, mybir.AxisListType
RADD, RMAX = bass.bass_isa.ReduceOp.add, bass.bass_isa.ReduceOp.max

QK_SLOT = {1: 3, 12: 0, 16: 1, 25: 2}
XT_SLOT = {3: 0, 5: 1}
V_SLOT = {7: 0, 10: 1}
WO_SLOT = {6: 0, 8: 1}
X2_SLOT = {11: 0, 13: 1}
Z_SLOT = 15
FF1_SLOT = {17 + m: m for m in range(KH // 2)}
FF2_SLOT = {25 + n: n for n in range(2 * TILES)}
A_STATS, A_NORM = {0: 0, 2: 1}, {1: 0, 3: 1}
Y_NORM, B_STATS, B_NORM = {8: 0, 10: 1}, {9: 0, 11: 1}, {10: 0, 12: 1}
LAG_T, LAG_PV = 2, 3
LAG_RB, LAG_O, LAG_OT = 1, 4, 5


def need(eng, sem, value):
    if isinstance(value, int) and value <= 0:
        return
    eng.wait_ge(sem, value)


def settled_wait(eng, consts, sem, value):
    if not isinstance(value, int):
        value = eng.to_reg(value)
    eng.wait_ge(consts, 1)
    eng.wait_ge(sem, value)


class Iteration:

    def __init__(self, t, p, first=False, last=False, before=False, after=False,
                 last2=False):
        self.t, self.p = t, p
        self.has_next = not (last or after)
        self.has_now = not (before or after)
        self.has_prev = not (before or first)
        self.has_next2 = self.has_next and not last2
        self.before = before


def run_iterations(eng, body):
    body(Iteration(-1, PER_SEQ - 1, before=True))
    body(Iteration(0, 0, first=True))
    body(Iteration(1, 1))
    n = NSTEP // PER_SEQ - 1
    with eng.Fori(0, n, 1) as i:
        for q in range(PER_SEQ):
            body(Iteration(i * PER_SEQ + (2 + q), (2 + q) % PER_SEQ))
    for t in range(2 + n * PER_SEQ, NSTEP):
        body(Iteration(t, t % PER_SEQ, last=(t == NSTEP - 1), last2=(t == NSTEP - 2)))
    body(Iteration(NSTEP, 0, after=True))


def lagged(it, slot, lag):
    j = slot - lag
    if j >= 0:
        return it.has_now, it.t, it.p, j
    return it.has_prev, it.t - 1, (it.p - 1) % PER_SEQ, j + SLOTS


def block_of(j):
    return j // (TILES * GROUP), j // GROUP % TILES, j % GROUP


def key_chunks(p, qc):
    c = p * TILES + qc
    return [(i, c - NKC + 1 + i) for i in range(NKC) if c - NKC + 1 + i >= 0]


def prepare(nc, A, W):
    with ExitStack() as ctx:
        def sb(name, shape, dt):
            return ctx.enter_context(nc.sbuf_tensor(name, shape, dt))

        def sem(name):
            return ctx.enter_context(nc.semaphore(name))

        stage = [sb(f"stage{i}", [P, 4 * D], F32) for i in range(3)]
        s_hi = [sb(f"s_hi{i}", [P, 4 * D], F16) for i in range(2)]
        s_lo = [sb(f"s_lo{i}", [P, 4 * D], F16) for i in range(2)]
        u_in = sb("u_in", [P, KH, RANK], F32)
        u_sc = sb("u_sc", [P, KH, RANK], F32)
        u_r = sb("u_r", [P, KH, RANK], F32)
        u_part = sb("u_part", [P, 3, KH, RANK], BF16)
        u_stack = sb("u_stack", [P, KH, LR], BF16)
        v_in = sb("v_in", [RANK, D], F32)
        fbT = sb("fbT", [RANK, RANK], F32)
        fb6 = sb("fb6", [RANK, LR], F32)
        vp = sb("vp", [P, KD, LR], F32)
        vsq = sb("vsq", [P, KD, RANK], F32)
        usq = sb("usq", [P, KH], F32)
        gate = sb("gate", [P, 1], F32)
        bqk = sb("bqk", [P, 2, KD], F32)
        red = sb("red", [P, 16], F32)
        redA = sb("redA", [P, 16], F32)
        vss = sb("vss", [P, 2], F32)
        bnd = sb("bnd", [P, 9], F32)
        p2 = sb("p2", [P, 9], F32)
        inv = sb("inv", [P, 9], F32)
        pow_in = sb("pow_in", [P, 2], F32)
        pow_ex = sb("pow_ex", [P, 2], F32)
        pow_out = sb("pow_out", [P, 2], F32)
        g23 = sb("g23", [P, 2], F32)
        s1 = sb("s1", [P, KH], F32)
        s2 = sb("s2", [P, KD], F32)
        h1 = sb("h1", [P, 2, KH], F32)
        h2 = sb("h2", [P, 2, KD], F32)
        fac = sb("fac", [P, KH], F32)
        s2c = sb("s2c", [P, KD], F32)
        sW = sb("sW", [P, 4], F32)
        ps = [ctx.enter_context(nc.psum_tensor(f"pp{i}", [P, 512], F32)) for i in range(4)]

        loaded = [sem(f"loaded{i}") for i in range(3)]
        s_small = sem("small_loaded")
        s_pool = sem("pool_ready")
        dch = sem("dve_step")
        s_stage_free = sem("stage_free")
        s_hi_done = sem("hi_done")
        s_act_hi = sem("weights_hi")
        s_scaled = sem("weights_scaled")
        s_bounds = sem("bound_inputs")
        s_pt = sem("prep_transposed")
        s_pe = sem("prep_evacuated")
        s_red = sem("red_ready")
        s_red_all = sem("red_all")
        block = ctx.enter_context(nc.Block())

        src = ([w.rearrange("(c p) i -> p c i", p=P) for w in (A["Wq"], A["Wk"], A["Wv"], A["Wo"])]
               + [A["w_fc"].rearrange("(m p) i -> p m i", p=P)[:, 4 * n:4 * n + 4, :] for n in range(4)]
               + [A["w_proj"].rearrange("(c p) h -> p c h", p=P)[:, n:n + 1, :] for n in range(4)])
        order = [0, 1, 2, 3] + [4, 5, 6, 7] + [8, 9, 10, 11] + [0, 1, 2, 3]
        NPIECE = len(order)

        def piece(n):
            return stage[n % 3][:, :]

        @block.sync
        def _(sp):
            sp.dma_start(u_in[:], A["u"].rearrange("(m p) r -> p m r", p=P)).then_inc(s_small, 16)
            sp.dma_start(v_in[:], A["v"]).then_inc(s_small, 16)
            with nc.allow_non_contiguous_dma(reason="256 words"):
                sp.dma_start(fbT[:], A["fast_b"].rearrange("a r -> r a")).then_inc(s_small, 16)
                sp.dma_start(bqk[:, 0, :], A["bq"].rearrange("(c p) -> p c", p=P)).then_inc(s_small, 16)
                sp.dma_start(bqk[:, 1, :], A["bk"].rearrange("(c p) -> p c", p=P)).then_inc(s_small, 16)
            sp.dma_start(gate[:], A["gate"].rearrange("(a b) -> a b", a=1).to_broadcast([P, 1])).then_inc(s_small, 16)
            sp.dma_start(W["bv"][:], A["bv"].rearrange("(a d) -> a d", a=1).to_broadcast([P, D])).then_inc(s_small, 16)
            sp.dma_start(W["bo"][:], A["bo"].rearrange("(a d) -> a d", a=1).to_broadcast([P, D])).then_inc(s_small, 16)
            for n in range(NPIECE):
                if n >= 3:
                    m = n - 3
                    sp.wait_ge(*((s_stage_free, m + 1) if m < 4 else (s_hi_done, m - 3)))
                a = src[order[n]]
                d = piece(n).rearrange("p (c i) -> p c i", c=a.shape[1])
                sp.dma_start(d, a).then_inc(loaded[n % 3], 16)

        @block.gpsimd
        def _(g):
            g.memset(W["idf"][:], 0.0)
            g.memset(W["mask"][:], 0.0)
            g.memset(W["nhalf"][:], -0.5).then_inc(W["consts"], 1)
            g.memset(W["zsel"][:], -1.0)
            g.memset(pow_ex[:], 0.5).then_inc(s_pool, 1)
            g.wait_ge(s_pool, 1)
            g.affine_select(out=W["idf"][:], in_=W["idf"][:], compare_op=ALU.not_equal, fill=1.0, base=0,
                            pattern=[[-1, P]], channel_multiplier=1)
            m0, m2 = W["mask"][:, 0:P], W["mask"][:, WIN - P:WIN]
            g.affine_select(out=m0, in_=m0, compare_op=ALU.is_gt, fill=NEG, base=0,
                            pattern=[[1, P]], channel_multiplier=-1)
            g.affine_select(out=m2, in_=m2, compare_op=ALU.is_ge, fill=NEG, base=0,
                            pattern=[[-1, P]], channel_multiplier=1)
            for col, group in ((0, 3), (1, 5)):
                zs = W["zsel"][:, col:col + 1]
                last = g.affine_select(out=zs, in_=zs, compare_op=ALU.is_ge, fill=0.0, base=-group * RANK,
                                       pattern=[[0, 1]], channel_multiplier=1)
            last.then_inc(s_pool, 1)
            g.wait_ge(s_pool, 2)
            g.tensor_copy(W["idh"][:], W["idf"][:])
            g.tensor_copy(W["idb"][:], W["idf"][:]).then_inc(s_pool, 1)
            g.wait_ge(s_red, 1)
            g.partition_all_reduce(redA[:, 0:9], red[:, 0:9], P, RMAX).then_inc(s_red_all, 1)
            g.wait_ge(s_red, 2)
            g.partition_all_reduce(vss[:, 1:2], vss[:, 0:1], P, RADD).then_inc(s_red_all, 1)
            g.wait_ge(s_bounds, 1)
            g.tensor_tensor(pow_out[:], pow_in[:], pow_ex[:], ALU.pow).then_inc(s_red_all, 1)

        jobs = (["vp"] + [("t1", n, h) for n in range(4) for h in range(2)]
                + [("t2", n, h) for n in range(4) for h in range(2)] + ["s2"]
                + [("u", h) for h in range(2)] + [("w", n, c) for n in range(4) for c in range(4)])

        @block.tensor
        def _(pe):
            pe.wait_ge(s_pool, 3)
            for n, job in enumerate(jobs):
                if n >= 4:
                    pe.wait_ge(s_pe, n - 3)
                b = ps[n % 4]
                bh = b[:, :].bitcast(F16)
                if job == "vp":
                    pe.wait_ge(dch, 1)
                    for k in range(KD):
                        last = pe.matmul(b[:, k * LR:(k + 1) * LR], v_in[:, k * P:(k + 1) * P], fb6[:],
                                         start=True, stop=True)
                elif job == "s2":
                    pe.wait_ge(s_red, 3)
                    for c in range(KD):
                        last = pe.transpose(b[:, c * P:(c + 1) * P], s2c[:, c:c + 1].to_broadcast([P, P]),
                                            W["idf"][:])
                elif job[0] == "t1":
                    _, n4, h = job
                    pe.wait_ge(s_hi_done, n4 + 1)
                    for k in range(KD):
                        for mm in range(2):
                            m = 2 * h + mm
                            last = pe.transpose(bh[:, k * 256 + mm * P:k * 256 + mm * P + P],
                                                s_hi[n4 % 2][:, m * D + k * P:m * D + k * P + P], W["idh"][:])
                elif job[0] == "t2":
                    _, c, h = job
                    pe.wait_ge(s_hi_done, 4 + c + 1)
                    for m in range(8):
                        last = pe.transpose(bh[:, m * P:m * P + P],
                                            s_hi[c % 2][:, (8 * h + m) * P:(8 * h + m + 1) * P], W["idh"][:])
                elif job[0] == "u":
                    h = job[1]
                    pe.wait_ge(s_red, 4)
                    bb = b[:, :].bitcast(BF16)
                    for m in range(8):
                        last = pe.transpose(bb[0:LR, m * P:m * P + P], u_stack[:, 8 * h + m, :], W["idb"][:])
                else:
                    _, w, c = job
                    pe.wait_ge(s_hi_done, 8 + w + 1)
                    for part, t in enumerate((s_hi, s_lo)):
                        for k in range(KD):
                            last = pe.transpose(bh[:, (part * KD + k) * P:(part * KD + k + 1) * P],
                                                t[w % 2][:, c * D + k * P:c * D + k * P + P], W["idh"][:])
                last.then_inc(s_pt, 1)

        @block.scalar
        def _(act):
            for w in range(4):
                act.wait_ge(s_scaled, w + 1)
                if w >= 2:
                    act.wait_ge(s_pt, len(jobs) - 16 + 4 * (w - 1))
                act.activation(s_hi[w % 2][:], piece(12 + w), ACT.Copy).then_inc(s_act_hi, 1)

        @block.vector
        def _(v):
            count = {}

            def then(ins, sem=dch):
                count[sem.name] = count.get(sem.name, 0) + 1
                ins.then_inc(sem, 1)
                v.wait_ge(sem, count[sem.name])

            def evacuate(n0, n1):
                for n in range(n0, n1):
                    job, b = jobs[n], ps[n % 4]
                    bh = b[:, :].bitcast(F16)
                    v.wait_ge(s_pt, n + 1)
                    if job == "vp":
                        ins = v.tensor_copy(vp[:].rearrange("p k c -> p (k c)"), b[:, 0:KD * LR])
                    elif job == "s2":
                        ins = v.tensor_copy(W["s2"][:], b[:, :])
                    elif job[0] == "t1":
                        m = 4 * job[1] + 2 * job[2]
                        ins = v.tensor_copy(W["t1"][:, :, m * P:(m + 2) * P],
                                            bh.rearrange("p (k c) -> p k c", k=KD))
                    elif job[0] == "t2":
                        _, c, h = job
                        ins = v.tensor_copy(W["t2"][:, 8 * h:8 * h + 8, c * P:(c + 1) * P],
                                            bh.rearrange("p (m c) -> p m c", m=8))
                    elif job[0] == "u":
                        h = job[1]
                        ins = v.tensor_copy(W["u"][:, 8 * h * P:(8 * h + 8) * P], b[0:LR, :].bitcast(BF16))
                    else:
                        _, w, c = job
                        ins = v.tensor_copy(
                            W["w"][:, w].rearrange("p a k o -> p (a k) o")[:, :, c * P:(c + 1) * P],
                            bh.rearrange("p (g c) -> p g c", g=2 * KD))
                    ins.then_inc(s_pe, 1)

            v.wait_ge(s_small, 16 * 8)
            then(v.tensor_copy(fb6[:].rearrange("p (g r) -> p g r", g=6),
                               fbT[:].rearrange("p (g r) -> p g r", g=1).to_broadcast([RANK, 6, RANK])))
            then(v.tensor_tensor(u_sc[:], u_in[:], u_in[:], ALU.mult))
            then(v.tensor_reduce(usq[:], u_sc[:], AX.X, ALU.add))
            v.tensor_reduce(red[:, 8:9], usq[:], AX.X, ALU.max)
            v.tensor_reduce(red[:, 4:6], bqk[:], AX.X, ALU.max, apply_absolute_value=True)
            v.tensor_reduce(red[:, 6:7], W["bv"][:], AX.X, ALU.max, apply_absolute_value=True)
            for n in range(12):
                v.wait_ge(loaded[n % 3], 16 * (n // 3 + 1))
                if n < 4:
                    v.tensor_reduce(red[:, n:n + 1], piece(n), AX.X, ALU.max,
                                    apply_absolute_value=True).then_inc(s_stage_free, 1)
                    continue
                m = n - 4
                s, h, w = (s1, h1, 4) if m < 4 else (s2, h2, 1)
                c0 = w * (m % 4)
                pc = piece(n).rearrange("p (c i) -> p c i", c=w)
                then(v.tensor_reduce(s[:, c0:c0 + w], pc, AX.X, ALU.add, apply_absolute_value=True))
                then(v.tensor_scalar(s[:, c0:c0 + w], s[:, c0:c0 + w], w / (4.0 * D), EPS, ALU.mult, ALU.max))
                v.tensor_scalar(h[:, 0, c0:c0 + w], s[:, c0:c0 + w], -0.5, None, ALU.mult)
                then(v.tensor_scalar(h[:, 1, c0:c0 + w], s[:, c0:c0 + w], 0.5, None, ALU.mult))
                if m == 1:
                    evacuate(0, 1)
                if m >= 2:
                    evacuate(2 * m - 3, 2 * m - 1)
                o = s_hi[m % 2][:].rearrange("p (c i) -> p c i", c=w)
                below = s_lo[m % 2][:].rearrange("p (c i) -> p c i", c=w)
                for c in range(w):
                    last = v.tensor_scalar(below[:, c], pc[:, c], h[:, 0, c0 + c:c0 + c + 1], None, ALU.is_lt)
                then(last)
                for c in range(w):
                    last = v.scalar_tensor_tensor(o[:, c], pc[:, c], h[:, 1, c0 + c:c0 + c + 1], below[:, c],
                                                  ALU.is_gt, ALU.subtract)
                then(last, s_hi_done)
                if m == 3:
                    then(v.tensor_reduce(red[:, 7:8], s1[:], AX.X, ALU.max), s_red)
            v.wait_ge(s_pe, 1)
            then(v.tensor_tensor(vsq[:], vp[:, :, 0:RANK], vp[:, :, 0:RANK], ALU.mult))
            then(v.tensor_reduce(vss[:, 0:1], vsq[:], AX.XY, ALU.add), s_red)
            v.wait_ge(s_red_all, 2)
            v.tensor_tensor(pow_in[:, 0:1], redA[:, 8:9], vss[:, 1:2], ALU.mult)
            then(v.tensor_copy(pow_in[:, 1:2], vss[:, 1:2]), s_bounds)
            v.tensor_copy(bnd[:, 0:4], redA[:, 0:4])
            v.scalar_tensor_tensor(bnd[:, 4:7], redA[:, 0:3], 1.01 * D, redA[:, 4:7], ALU.mult, ALU.add)
            then(v.scalar_tensor_tensor(g23[:, 0:1], gate[:], -1.0, gate[:], ALU.mult, ALU.max))
            v.wait_ge(s_red_all, 3)
            v.tensor_scalar(bnd[:, 7:8], pow_out[:, 1:2], 1.01, None, ALU.mult)
            then(v.scalar_tensor_tensor(g23[:, 1:2], g23[:, 0:1], 23.0, pow_out[:, 0:1], ALU.mult, ALU.mult))
            then(v.scalar_tensor_tensor(bnd[:, 8:9], redA[:, 7:8], 1.01 * D, g23[:, 1:2], ALU.mult, ALU.add))
            then(v.tensor_scalar(bnd[:], bnd[:], 1e-20, None, ALU.max))
            then(v.tensor_scalar(p2[:].bitcast(U32), bnd[:].bitcast(U32), 0x7F800000, None, ALU.bitwise_and))
            then(v.reciprocal(inv[:], p2[:]))
            then(v.tensor_scalar(sW[:], inv[:, 0:4], 2.0 ** 14, None, ALU.mult))
            c = W["c"]
            v.tensor_tensor(c[:, 0:3], inv[:, 4:7], p2[:, 0:3], ALU.mult)
            v.tensor_tensor(c[:, 3:4], p2[:, 4:5], p2[:, 5:6], ALU.mult)
            v.tensor_scalar(c[:, 5:8], inv[:, 4:7], 2.0 ** 14, None, ALU.mult)
            v.tensor_scalar(c[:, 8:9], inv[:, 8:9], 2.0 ** 6 / XS, None, ALU.mult)
            v.tensor_tensor(c[:, 9:10], p2[:, 8:9], p2[:, 8:9], ALU.mult)
            v.tensor_scalar(c[:, 10:11], inv[:, 7:8], 2.0 ** 14, None, ALU.mult)
            v.tensor_scalar(c[:, 11:12], p2[:, 7:8], 2.0 ** -14, gate[:, 0:1], ALU.mult, ALU.mult)
            v.reciprocal(fac[:], s1[:])
            then(v.tensor_tensor(c[:, 4:5], p2[:, 6:7], p2[:, 3:4], ALU.mult))
            v.tensor_scalar(c[:, 0:3], c[:, 0:3], 1.0 / XS, None, ALU.mult)
            v.tensor_scalar(c[:, 3:4], c[:, 3:4], -(float(HD) ** -0.5) * 2.0 ** -28, None, ALU.mult)
            v.tensor_scalar(c[:, 4:5], c[:, 4:5], 2.0 ** -28, None, ALU.mult)
            v.tensor_scalar(W["bqs"][:, 0, :], bqk[:, 0, :], c[:, 5:6], None, ALU.mult)
            v.tensor_scalar(W["bqs"][:, 1, :], bqk[:, 1, :], c[:, 6:7], None, ALU.mult)
            v.tensor_scalar(W["bv"][:], W["bv"][:], c[:, 7:8], None, ALU.mult)
            v.tensor_scalar(W["c1"][:], s1[:], c[:, 8:9], None, ALU.mult)
            v.tensor_scalar(fac[:], fac[:], c[:, 11:12], None, ALU.mult)
            then(v.tensor_scalar(vp[:], vp[:], c[:, 10:11], None, ALU.mult))
            evacuate(13, 17)
            v.tensor_scalar(s2c[:], s2[:], c[:, 9:10], 2.0 ** -12, ALU.mult, ALU.mult).then_inc(s_red, 1)
            then(v.tensor_copy(W["v"][:, 0], vp[:]))
            v.tensor_tensor(W["v"][:, 1], vp[:], W["v"][:, 0], ALU.subtract)
            then(v.tensor_tensor(u_sc[:], u_in[:],
                                 fac[:].rearrange("p (m o) -> p m o", o=1).to_broadcast([P, KH, RANK]), ALU.mult))
            then(v.tensor_copy(u_part[:, 0], u_sc[:]))
            then(v.tensor_tensor(u_r[:], u_sc[:], u_part[:, 0], ALU.subtract))
            then(v.tensor_copy(u_part[:, 1], u_r[:]))
            then(v.tensor_tensor(u_part[:, 2], u_r[:], u_part[:, 1], ALU.subtract))
            for g, part in enumerate((0, 1, 2, 0, 1, 0)):
                last = v.tensor_copy(u_stack[:, :, g * RANK:(g + 1) * RANK], u_part[:, part])
            last.then_inc(s_red, 1)
            evacuate(17, 20)
            for w in range(4):
                n = 12 + w
                v.wait_ge(loaded[n % 3], 16 * (n // 3 + 1))
                then(v.tensor_scalar(piece(n), piece(n), sW[:, w:w + 1], None, ALU.mult), s_scaled)
                if w >= 2:
                    evacuate(20 + 4 * (w - 2), 20 + 4 * (w - 1))
                v.wait_ge(s_act_hi, w + 1)
                v.tensor_tensor(s_lo[w % 2][:], piece(n), s_hi[w % 2][:], ALU.subtract).then_inc(s_hi_done, 1)
            evacuate(28, 36)


def steps(nc, A, W, out):
    with ExitStack() as ctx:
        def sb(name, shape, dt):
            return ctx.enter_context(nc.sbuf_tensor(name, shape, dt))

        def bank(name):
            return ctx.enter_context(nc.psum_tensor(name, [P, 512], F32))

        def sem(name):
            return ctx.enter_context(nc.semaphore(name))

        xa = sb("xa", [P, TILES, D], F32)
        xn = sb("xn", [P, D], F32)
        xh, xl = sb("xh", [P, D], F16), sb("xl", [P, D], F16)
        xT = sb("xT", [P, 2, KD, STEP], F16)
        qk32 = sb("qk32", [P, 2, STEP], F32)
        qkp = sb("qkp", [P, 2, 2, STEP], F16)
        Q3 = sb("Q3", [ST, HEADS, STEP], F16)
        K3 = sb("K3", [ST, HEADS, RING], F16)
        V = sb("V", [P, SEQ // P, D], F32)
        NSM, NPT = 4, 8
        Sm = sb("Sm", [P, NSM, WIN], F32)
        nmax = sb("nmax", [P, 8], F32)
        sums = sb("sums", [P, 2, TILES, GROUP], F32)
        PTs = sb("PTs", [P, NPT, WIN], F32)
        rb = sb("rb", [P, TILES, GROUP, HD], F32)
        Rs = sb("Rs", [P, STEP], F32)
        o32 = sb("o32", [P, STEP], F32)
        OT = sb("OT", [P, 2, NGROUP, STEP], F16)
        xr = sb("xr", [P, TILES, D], F32)
        yb = sb("yb", [P, D], F32)
        x1 = sb("x1", [P, TILES, D], F32)
        x2n = sb("x2n", [P, D], F32)
        x2h, x2l = sb("x2h", [P, D], F16), sb("x2l", [P, D], F16)
        x2T = sb("x2T", [P, 2, KD, STEP], F16)
        z_h, z_m, z6 = (sb(n, [LR, STEP], BF16) for n in ("z_h", "z_m", "z6"))
        z_r = sb("z_r", [LR, STEP], F32)
        r32, sq32 = sb("r32", [P, 2 * STEP], F32), sb("sq32", [P, 2 * STEP], F32)
        r2 = sb("r2", [P, 2, KH, STEP], F16)
        yc = sb("yc", [P, TILES, D], F32)
        lnst = sb("lnst", [P, 4, 6], F32)
        lnmv = sb("lnmv", [P, 4, 2], F32)
        lnve = sb("lnve", [P, 4, 1], F32)
        lnrs = sb("lnrs", [P, 4, 2], F32)

        Sb = [bank("S0"), bank("S1")]
        PTb, Ob = bank("PTb"), bank("Ob")
        Fb = [bank("F0"), bank("F1")]
        Ab, Cb = bank("Ab"), bank("Cb")

        names = """xa_in0 xa_in1 a_st a_mv a_ve a_rs a_xn a_xh a_xl
            A_full A_free  qk_hi_done qk_lo_done stacked0 stacked1 stacked2 stacked3
            S_full S_done S_exp T_full PT_copied_act PT_copied_dve PT_used rb_done O_full Rs_done o32_done
            OT_hi OT_lo
            xr_in0 xr_in1 y_done y_st y_mv y_ve y_rs y_n x1_done b_st b_mv b_ve b_rs b_xn b_xh b_xl
            C_full C_free z_hi z_r1 z_mid z_done F_full0 F_full1 F_free0 F_free1 relu_done r2_hi r2_sq r2_lo
            c_y c_st c_mv c_ve c_rs c_n c_out stored0 stored1""".split()
        M = {n: sem(n) for n in names}

        def copied(eng, t, j):
            need(eng, M["PT_copied_dve" if j % 2 else "PT_copied_act"], t * (SLOTS // 2) + j // 2 + 1)

        NA = 8
        NC = 5
        NF = 5

        def xrow(ap, t, i):
            if isinstance(t, int):
                r0 = t * STEP + i * P
                return ap[r0:r0 + P, :]
            return ap[bass.ds(t * STEP + i * P, P), :]

        block = ctx.enter_context(nc.Block())

        @block.sync
        def _(sp):
            def load_x(t, i):
                need(sp, M["a_xn"], (t - 1) * TILES + i + 1)
                sp.dma_start(xa[:, i, :], xrow(A["x"], t, i)).then_inc(M[f"xa_in{i}"], 16)

            def stack(t, p, hg):
                slot = (p * TILES % (RING // P)) * P
                sp.wait_ge(M["qk_hi_done"], t * NGROUP + hg + 1)
                sp.wait_ge(M["qk_lo_done"], t * NGROUP + hg + 1)
                for r in range(GROUP):
                    h, rows = hg * GROUP + r, slice(r * HD, (r + 1) * HD)
                    for term, (qpart, kpart) in enumerate(((0, 0), (0, 1), (1, 0))):
                        dst = slice(term * HD, (term + 1) * HD)
                        sp.dma_start(Q3[dst, h, :], qkp[rows, qpart, 0, :]).then_inc(M[f"stacked{hg}"], 16)
                        sp.dma_start(K3[dst, h, slot:slot + STEP],
                                     qkp[rows, kpart, 1, :]).then_inc(M[f"stacked{hg}"], 16)

            def body(it):
                if it.before:
                    for i in range(TILES):
                        load_x(0, i)
                for s in range(SLOTS):
                    if s - 2 in QK_SLOT:
                        hg = QK_SLOT[s - 2]
                        if hg == 3 and it.has_now:
                            stack(it.t, it.p, hg)
                        if hg != 3 and it.has_next:
                            stack(it.t + 1, (it.p + 1) % PER_SEQ, hg)
                    if s == 4 and it.has_prev:
                        for i in range(TILES):
                            need(sp, M["x1_done"], (it.t - 2) * TILES + i + 1)
                            sp.dma_start(xr[:, i, :], xrow(A["x"], it.t - 1, i)).then_inc(M[f"xr_in{i}"], 16)
                    if s == 5 and it.has_next2:
                        for i in range(TILES):
                            load_x(it.t + 2, i)
                if it.has_prev:
                    for i in range(TILES):
                        sp.wait_ge(M["c_out"], (it.t - 1) * TILES + i + 1)
                        sp.dma_start(xrow(out, it.t - 1, i), yc[:, i, :]).then_inc(M[f"stored{i}"], 16)

            run_iterations(sp, body)
            for i in range(TILES):
                sp.wait_ge(M[f"stored{i}"], 16 * NSTEP)

        @block.tensor
        def _(pe):
            def scores(t, p, j):
                hg, qc, r = block_of(j)
                h = hg * GROUP + r
                if qc == 0 and r == 0:
                    pe.wait_ge(M[f"stacked{hg}"], (t + 1) * 6 * GROUP * 16)
                need(pe, M["S_done"], t * SLOTS + j - 1)
                kc = key_chunks(p, qc)
                runs = []
                for place, c in kc:
                    if runs and (c % (RING // P)) == runs[-1][1] + runs[-1][2]:
                        runs[-1][2] += 1
                    else:
                        runs.append([place, c % (RING // P), 1])
                for place, slot, n in runs:
                    mm = pe.matmul(Sb[j % 2][:, place * P:(place + n) * P], Q3[:, h, qc * P:(qc + 1) * P],
                                   K3[:, h, slot * P:(slot + n) * P], start=True, stop=True,
                                   skip_group_check=True)
                mm.then_inc(M["S_full"], 1)

            def transposes(t, p, j):
                hg, qc, r = block_of(j)
                pe.wait_ge(M["S_exp"], t * SLOTS + j + 1)
                copied(pe, t, j - 1)
                for place, _ in key_chunks(p, qc):
                    mm = pe.transpose(PTb[:, place * P:(place + 1) * P],
                                      Sm[:, j % NSM, place * P:(place + 1) * P], W["idf"][:])
                mm.then_inc(M["T_full"], 1)

            def weighted_values(t, p, g):
                hg, qc = g // TILES, g % TILES
                copied(pe, t, GROUP * g + GROUP - 1)
                copied(pe, t, GROUP * g + GROUP - 2)
                if qc == 0:
                    need(pe, M["o32_done"], t * NGROUP + hg)
                pe.wait_ge(M["A_free"], t * NA + 2 + qc + 1)
                kc = key_chunks(p, qc)
                for n, (place, c) in enumerate(kc):
                    for r in range(GROUP):
                        j = g * GROUP + r
                        mm = pe.matmul(Ob[r * HD:(r + 1) * HD, qc * P:(qc + 1) * P],
                                       V[:, c, (hg * GROUP + r) * HD:(hg * GROUP + r + 1) * HD],
                                       PTs[:, j % NPT, place * P:(place + 1) * P],
                                       start=(n == 0), stop=(n == len(kc) - 1), skip_group_check=True)
                mm.then_inc(M["PT_used"], 1)

            def reciprocal_rows(t, hg):
                pe.wait_ge(M["rb_done"], t * NGROUP + hg + 1)
                for qc in range(TILES):
                    mm = pe.transpose(Ob[:, STEP + qc * P:STEP + (qc + 1) * P],
                                      rb[:, qc].rearrange("p r d -> p (r d)"), W["idf"][:])
                mm.then_inc(M["O_full"], 1)

            def product3(outp, a, b):
                n = 0
                for pa, pb in ((0, 0), (0, 1), (1, 0)):
                    for k in range(KD):
                        mm = pe.matmul(outp, a(pa, k), b(pb, k), start=(n == 0), stop=(n == 3 * KD - 1),
                                       skip_group_check=True)
                        n += 1
                return mm

            def a_transposes(t, i):
                need(pe, M["A_free"], t * NA + i)
                pe.wait_ge(M["a_xh"], t * TILES + i + 1)
                pe.wait_ge(M["a_xl"], t * TILES + i + 1)
                bh = Ab[:, :].bitcast(F16)
                for part, x in enumerate((xh, xl)):
                    for k in range(KD):
                        mm = pe.transpose(bh[:, (part * KD + k) * P:(part * KD + k + 1) * P],
                                          x[:, k * P:(k + 1) * P], W["idh"][:])
                mm.then_inc(M["A_full"], 1)

            def values(t, i):
                need(pe, M["A_free"], t * NA + 2 + i)
                mm = product3(Ab[:, :], lambda a, k: xT[:, a, k, i * P:(i + 1) * P],
                              lambda a, k: W["w"][:, 2, a, k, :])
                mm.then_inc(M["A_full"], 1)

            def queries_keys(t, hg):
                need(pe, M["A_free"], t * NA + 4 + hg)
                for w in range(2):
                    mm = product3(Ab[:, w * STEP:(w + 1) * STEP],
                                  lambda a, k: W["w"][:, w, a, k, hg * P:(hg + 1) * P],
                                  lambda a, k: xT[:, a, k, :])
                mm.then_inc(M["A_full"], 1)

            def out_projection(t, i):
                need(pe, M["C_free"], t * (NC - 1) + i)
                need(pe, M["z_r1"], t) if i == 0 else None
                pe.wait_ge(M["OT_hi"], (t + 1) * NGROUP)
                pe.wait_ge(M["OT_lo"], (t + 1) * NGROUP)
                mm = product3(Cb[:, :], lambda a, k: OT[:, a, k, i * P:(i + 1) * P],
                              lambda a, k: W["w"][:, 3, a, k, :])
                mm.then_inc(M["C_full"], 1)

            def c_transposes(t, i):
                need(pe, M["C_free"], t * (NC - 1) + 2 + i)
                pe.wait_ge(M["b_xh"], t * TILES + i + 1)
                pe.wait_ge(M["b_xl"], t * TILES + i + 1)
                bh = Cb[:, :].bitcast(F16)
                for part, x in enumerate((x2h, x2l)):
                    for k in range(KD):
                        mm = pe.transpose(bh[:, (part * KD + k) * P:(part * KD + k + 1) * P],
                                          x[:, k * P:(k + 1) * P], W["idh"][:])
                mm.then_inc(M["C_full"], 1)

            def low_rank(t):
                need(pe, M["C_free"], (t + 1) * (NC - 1))
                mm = product3(Cb[0:LR, 0:STEP], lambda a, k: W["v"][:, a, k, :], lambda a, k: x2T[:, a, k, :])
                mm.then_inc(M["C_full"], 1)

            def hidden(t, m):
                b = m % 2
                need(pe, M[f"F_free{b}"], t * NF + m // 2)
                if m == 0:
                    pe.wait_ge(M["z_done"], t + 1)
                for half in range(2):
                    mc = 2 * m + half
                    o = Fb[b][:, half * STEP:(half + 1) * STEP]
                    for k in range(KD):
                        for part in range(2):
                            pe.matmul(o, W["t1"][:, k, mc * P:(mc + 1) * P], x2T[:, part, k, :],
                                      start=(k == 0 and part == 0), stop=False, skip_group_check=True)
                    mm = pe.matmul(o, W["u"][:, mc * P:(mc + 1) * P], z6[:], start=False, stop=True,
                                   skip_group_check=True)
                mm.then_inc(M[f"F_full{b}"], 1)

            def ff_out(t, n):
                i, q = n // 2, n % 2
                if q == 0:
                    need(pe, M[f"F_free{i}"], t * NF + 4)
                if i == 0:
                    pe.wait_ge(M["r2_lo"], t * (KH // 2) + (q + 1) * KH // 4)
                    pe.wait_ge(M["r2_hi"], t * (KH // 2) + (q + 1) * KH // 4)
                for m in range(q * KH // 2, (q + 1) * KH // 2):
                    for part in range(2):
                        mm = pe.matmul(Fb[i][:, :], r2[:, part, m, i * P:(i + 1) * P], W["t2"][:, m, :],
                                       start=(m == 0 and part == 0), stop=(m == KH - 1 and part == 1),
                                       skip_group_check=True)
                if q == 1:
                    mm.then_inc(M[f"F_full{i}"], 1)

            def body(it):
                nxt, now, prev = it.has_next, it.has_now, it.has_prev
                for s in range(SLOTS):
                    if now:
                        scores(it.t, it.p, s)
                    ok, t, p, j = lagged(it, s, LAG_T)
                    if ok:
                        transposes(t, p, j)
                    ok, t, p, j = lagged(it, s, LAG_PV)
                    if ok and j % GROUP == GROUP - 1:
                        weighted_values(t, p, j // GROUP)
                        if j // GROUP % TILES == TILES - 1:
                            reciprocal_rows(t, j // GROUP // TILES)
                    if s in XT_SLOT and nxt:
                        a_transposes(it.t + 1, XT_SLOT[s])
                    if s in V_SLOT and nxt:
                        values(it.t + 1, V_SLOT[s])
                    if s in QK_SLOT and (now if QK_SLOT[s] == 3 else nxt):
                        queries_keys(it.t if QK_SLOT[s] == 3 else it.t + 1, QK_SLOT[s])
                    if prev:
                        if s in WO_SLOT:
                            out_projection(it.t - 1, WO_SLOT[s])
                        if s in X2_SLOT:
                            c_transposes(it.t - 1, X2_SLOT[s])
                        if s == Z_SLOT:
                            low_rank(it.t - 1)
                        if s in FF1_SLOT:
                            hidden(it.t - 1, FF1_SLOT[s])
                        if s in FF2_SLOT:
                            ff_out(it.t - 1, FF2_SLOT[s])

            run_iterations(pe, body)

        @block.scalar
        def _(act):
            def exponentials(t, p, j):
                hg, qc, r = block_of(j)
                c0 = key_chunks(p, qc)[0][0] * P
                act.wait_ge(M["S_done"], t * SLOTS + j + 1)
                blk = Sm[:, j % NSM, c0:WIN]
                act.activation(blk, blk, ACT.Exp, bias=nmax[:, j % 8:j % 8 + 1], scale=-1.0,
                               accum_out=sums[:, hg % 2, qc, r:r + 1]).then_inc(M["S_exp"], 1)

            def copy_transposed(t, p, j):
                c0 = key_chunks(p, block_of(j)[1])[0][0] * P
                act.wait_ge(M["T_full"], t * SLOTS + j + 1)
                need(act, M["PT_used"], t * (SLOTS // GROUP) + (j - NPT) // GROUP + 1)
                act.activation(PTs[:, j % NPT, c0:WIN], PTb[:, c0:WIN], ACT.Copy).then_inc(M["PT_copied_act"], 1)

            def sum_rows(t, hg):
                act.wait_ge(M["O_full"], t * NGROUP + hg + 1)
                need(act, M["o32_done"], t * NGROUP + hg)
                act.activation(Rs[:], Ob[:, STEP:2 * STEP], ACT.Copy).then_inc(M["Rs_done"], 1)

            def out_hi(t, hg):
                act.wait_ge(M["o32_done"], t * NGROUP + hg + 1)
                need(act, M["C_full"], (t - 1) * NC + 2)
                act.activation(OT[:, 0, hg, :], o32[:], ACT.Copy).then_inc(M["OT_hi"], 1)

            def a_hi(t, i):
                act.wait_ge(M["a_xn"], t * TILES + i + 1)
                need(act, M["A_full"], t * NA + i if i else (t - 1) * NA + TILES)
                act.activation(xh[:], xn[:], ACT.Copy).then_inc(M["a_xh"], 1)

            def qk_bias(t, hg):
                act.wait_ge(M["A_full"], t * NA + 4 + hg + 1)
                need(act, M["qk_hi_done"], t * NGROUP + hg)
                need(act, M["qk_lo_done"], t * NGROUP + hg)
                act.activation(qk32[:, 0, :], Ab[:, 0:STEP], ACT.Identity, bias=W["bqs"][:, 0, hg:hg + 1],
                               scale=W["c"][:, 0:1])
                act.activation(qk32[:, 1, :], Ab[:, STEP:2 * STEP], ACT.Identity,
                               bias=W["bqs"][:, 1, hg:hg + 1], scale=W["c"][:, 1:2]).then_inc(M["A_free"], 1)

            def b_hi(t, i):
                act.wait_ge(M["b_xn"], t * TILES + i + 1)
                need(act, M["C_full"], t * NC + 2 + i if i else (t - 1) * NC + 2 + TILES)
                act.activation(x2h[:], x2n[:], ACT.Copy).then_inc(M["b_xh"], 1)

            def z_first(t):
                act.wait_ge(M["C_full"], t * NC + 5)
                act.activation(z_h[:], Cb[0:LR, 0:STEP], ACT.Copy).then_inc(M["z_hi"], 1)

            def z_second(t):
                act.wait_ge(M["z_r1"], t + 1)
                act.activation(z_m[:], z_r[:], ACT.Copy).then_inc(M["z_mid"], 1)

            def relu_square(t, m):
                b = m % 2
                act.wait_ge(M[f"F_full{b}"], t * NF + m // 2 + 1)
                need(act, M["r2_sq"], t * (KH // 2) + m)
                need(act, M["r2_hi"], t * (KH // 2) + m)
                for half in range(2):
                    ins = act.activation(r32[:, half * STEP:(half + 1) * STEP],
                                         Fb[b][:, half * STEP:(half + 1) * STEP], ACT.Relu,
                                         scale=W["c1"][:, 2 * m + half:2 * m + half + 1])
                ins.then_inc(M[f"F_free{b}"], 1)
                act.wait_ge(M[f"F_free{b}"], t * NF + m // 2 + 1)
                need(act, M["F_full1"], t * NF)
                act.activation(r2[:, 0, 2 * m:2 * m + 2, :].rearrange("p m n -> p (m n)"), r32[:],
                               ACT.Square).then_inc(M["r2_hi"], 1)

            def body(it):
                for s in range(SLOTS):
                    if it.has_now:
                        exponentials(it.t, it.p, s)
                    ok, t, p, j = lagged(it, s, LAG_T)
                    if ok and j % 2 == 0:
                        copy_transposed(t, p, j)
                    ok, t, p, j = lagged(it, s, LAG_O)
                    if ok and j % (TILES * GROUP) == TILES * GROUP - 1:
                        sum_rows(t, block_of(j)[0])
                    ok, t, p, j = lagged(it, s, LAG_OT)
                    if ok and j % (TILES * GROUP) == TILES * GROUP - 1:
                        out_hi(t, block_of(j)[0])
                    if s in A_NORM and it.has_next:
                        a_hi(it.t + 1, A_NORM[s])
                    if s - 1 in QK_SLOT:
                        hg = QK_SLOT[s - 1]
                        if it.has_now if hg == 3 else it.has_next:
                            qk_bias(it.t if hg == 3 else it.t + 1, hg)
                    if it.has_prev:
                        if s in B_NORM:
                            b_hi(it.t - 1, B_NORM[s])
                        if s == Z_SLOT:
                            z_first(it.t - 1)
                        if s == Z_SLOT + 1:
                            z_second(it.t - 1)
                        if s - 1 in FF1_SLOT:
                            relu_square(it.t - 1, FF1_SLOT[s - 1])

            run_iterations(act, body)

        @block.vector
        def _(v):
            def masked_scores(t, p, j):
                hg, qc, r = block_of(j)
                c0 = key_chunks(p, qc)[0][0] * P
                need(v, M["T_full"], t * SLOTS + j - NSM + 1)
                settled_wait(v, W["consts"], M["S_full"], t * SLOTS + j + 1)
                v.tensor_tensor_reduce(Sm[:, j % NSM, c0:WIN], Sb[j % 2][:, c0:WIN], W["mask"][:, c0:WIN],
                                       W["c"][:, 3:4], 3e38, ALU.add, ALU.min,
                                       nmax[:, j % 8:j % 8 + 1]).then_inc(M["S_done"], 1)

            def copy_transposed(t, p, j):
                c0 = key_chunks(p, block_of(j)[1])[0][0] * P
                v.wait_ge(M["T_full"], t * SLOTS + j + 1)
                need(v, M["PT_used"], t * (SLOTS // GROUP) + (j - NPT) // GROUP + 1)
                v.tensor_copy(PTs[:, j % NPT, c0:WIN], PTb[:, c0:WIN]).then_inc(M["PT_copied_dve"], 1)

            def reciprocals(t, hg):
                v.wait_ge(M["S_exp"], t * SLOTS + (hg + 1) * TILES * GROUP)
                need(v, M["O_full"], t * NGROUP + hg)
                v.reciprocal(rb[:].rearrange("p a r d -> p (a r) d"),
                             sums[:, hg % 2].rearrange("p a (r o) -> p (a r) o", o=1)
                             .to_broadcast([P, TILES * GROUP, HD])).then_inc(M["rb_done"], 1)

            def normalised(t, hg):
                v.wait_ge(M["Rs_done"], t * NGROUP + hg + 1)
                need(v, M["OT_hi"], t * NGROUP + hg)
                need(v, M["OT_lo"], t * NGROUP + hg)
                v.tensor_tensor(o32[:], Ob[:, 0:STEP], Rs[:], ALU.mult).then_inc(M["o32_done"], 1)

            def ln_stats(k, row, x, n):
                v.bn_stats(lnst[:, row, :], x).then_inc(M[k + "_st"], 1)
                settled_wait(v, W["consts"], M[k + "_st"], n + 1)
                v.bn_aggr(lnmv[:, row, :], lnst[:, row, :]).then_inc(M[k + "_mv"], 1)
                v.wait_ge(M[k + "_mv"], n + 1)

            def a_stats(t, i):
                n = t * TILES + i
                v.wait_ge(M[f"xa_in{i}"], (t + 1) * 16)
                ln_stats("a", 0, xa[:, i, :], n)
                v.tensor_scalar(lnve[:, 0, :], lnmv[:, 0, 1:2], EPS, XS ** -2, ALU.add,
                                ALU.mult).then_inc(M["a_ve"], 1)

            def a_norm(t, i):
                n = t * TILES + i
                v.wait_ge(M["a_rs"], n + 1)
                need(v, M["a_xh"], n)
                need(v, M["a_xl"], n)
                v.tensor_scalar(xn[:], xa[:, i, :], lnmv[:, 0, 0:1], lnrs[:, 0, 0:1], ALU.subtract,
                                ALU.mult).then_inc(M["a_xn"], 1)

            def a_evacuate(t, i):
                v.wait_ge(M["A_full"], t * NA + i + 1)
                v.tensor_copy(xT[:].rearrange("p a k n -> p (a k) n")[:, :, i * P:(i + 1) * P],
                              Ab[:, :].bitcast(F16).rearrange("p (g n) -> p g n", g=2 * KD)
                              ).then_inc(M["A_free"], 1)

            def v_evacuate(t, p, i):
                v.wait_ge(M["A_full"], t * NA + 2 + i + 1)
                need(v, M["PT_used"], (t - 2) * (SLOTS // GROUP))
                v.scalar_tensor_tensor(V[:, p * TILES + i, :], Ab[:, :], W["c"][:, 2:3], W["bv"][:],
                                       ALU.mult, ALU.add).then_inc(M["A_free"], 1)

            def qk_hi(t, hg):
                v.wait_ge(M["A_free"], t * NA + 4 + hg + 1)
                b, c = (hg - 1, t + 1) if hg else (NGROUP - 1, t)
                need(v, M[f"stacked{b}"], c * 6 * GROUP * 16)
                v.tensor_copy(qkp[:, 0], qk32[:]).then_inc(M["qk_hi_done"], 1)

            def y_evacuate(t, i):
                n = t * TILES + i
                v.wait_ge(M["C_full"], t * NC + i + 1)
                need(v, M["x1_done"], n)
                v.scalar_tensor_tensor(yb[:], Cb[:, :], W["c"][:, 4:5], W["bo"][:], ALU.mult,
                                       ALU.add).then_inc(M["C_free"], 1)
                v.wait_ge(M["C_free"], t * (NC - 1) + i + 1)
                ln_stats("y", 1, yb[:], n)
                v.tensor_scalar(lnve[:, 1, :], lnmv[:, 1, 1:2], EPS, None, ALU.add).then_inc(M["y_ve"], 1)

            def y_norm(t, i):
                n = t * TILES + i
                v.wait_ge(M["y_rs"], n + 1)
                v.tensor_scalar(yb[:], yb[:], lnmv[:, 1, 0:1], lnrs[:, 1, 0:1], ALU.subtract,
                                ALU.mult).then_inc(M["y_n"], 1)

            def b_stats(t, i):
                n = t * TILES + i
                v.wait_ge(M["x1_done"], n + 1)
                ln_stats("b", 2, x1[:, i, :], n)
                v.tensor_scalar(lnve[:, 2, :], lnmv[:, 2, 1:2], EPS, XS ** -2, ALU.add,
                                ALU.mult).then_inc(M["b_ve"], 1)

            def b_norm(t, i):
                n = t * TILES + i
                v.wait_ge(M["b_rs"], n + 1)
                need(v, M["b_xh"], n)
                need(v, M["b_xl"], n)
                v.tensor_scalar(x2n[:], x1[:, i, :], lnmv[:, 2, 0:1], lnrs[:, 2, 0:1], ALU.subtract,
                                ALU.mult).then_inc(M["b_xn"], 1)

            def b_evacuate(t, i):
                v.wait_ge(M["C_full"], t * NC + 2 + i + 1)
                need(v, M["F_full1"], t * NF)
                v.tensor_copy(x2T[:].rearrange("p a k n -> p (a k) n")[:, :, i * P:(i + 1) * P],
                              Cb[:, :].bitcast(F16).rearrange("p (g n) -> p g n", g=2 * KD)
                              ).then_inc(M["C_free"], 1)

            def z_rest(t):
                v.wait_ge(M["z_hi"], t + 1)
                need(v, M["z_done"], t)
                v.scalar_tensor_tensor(z_r[:], z_h[:], W["zsel"][0:LR, 0:1], Cb[0:LR, 0:STEP], ALU.mult,
                                       ALU.add).then_inc(M["z_r1"], 1)

            def z_last(t):
                v.wait_ge(M["z_mid"], t + 1)
                need(v, M["F_full1"], t * NF)
                v.scalar_tensor_tensor(z6[:], z_m[:], W["zsel"][0:LR, 1:2], z_r[:], ALU.mult,
                                       ALU.add).then_inc(M["z_done"], 1)

            def square_lo(t, m):
                v.wait_ge(M["r2_sq"], t * (KH // 2) + m + 1)
                v.wait_ge(M["r2_hi"], t * (KH // 2) + m + 1)
                v.tensor_tensor(r2[:, 1, 2 * m:2 * m + 2, :].rearrange("p m n -> p (m n)"), sq32[:],
                                r2[:, 0, 2 * m:2 * m + 2, :].rearrange("p m n -> p (m n)"),
                                ALU.subtract).then_inc(M["r2_lo"], 1)

            def c_evacuate(t, i):
                n = t * TILES + i
                v.wait_ge(M[f"F_full{i}"], t * NF + 5)
                need(v, M[f"stored{i}"], t * 16)
                v.tensor_tensor(yc[:, i, :], Fb[i][:, :], W["s2"][:], ALU.mult).then_inc(M[f"F_free{i}"], 1)
                v.wait_ge(M[f"F_free{i}"], t * NF + 5)
                ln_stats("c", 3, yc[:, i, :], n)
                v.tensor_scalar(lnve[:, 3, :], lnmv[:, 3, 1:2], EPS, None, ALU.add).then_inc(M["c_ve"], 1)

            def c_norm(t, i):
                n = t * TILES + i
                v.wait_ge(M["c_rs"], n + 1)
                v.tensor_scalar(yc[:, i, :], yc[:, i, :], lnmv[:, 3, 0:1], lnrs[:, 3, 0:1], ALU.subtract,
                                ALU.mult).then_inc(M["c_n"], 1)

            def body(it):
                for s in range(SLOTS):
                    if it.has_now:
                        masked_scores(it.t, it.p, s)
                    ok, t, p, j = lagged(it, s, LAG_T)
                    if ok and j % 2:
                        copy_transposed(t, p, j)
                    ok, t, p, j = lagged(it, s, LAG_RB)
                    if ok and j % (TILES * GROUP) == TILES * GROUP - 1:
                        reciprocals(t, block_of(j)[0])
                    ok, t, p, j = lagged(it, s, LAG_O)
                    if ok and j % (TILES * GROUP) == TILES * GROUP - 1:
                        normalised(t, block_of(j)[0])
                    if it.has_next:
                        t = it.t + 1
                        if s in A_STATS:
                            a_stats(t, A_STATS[s])
                        if s in A_NORM:
                            a_norm(t, A_NORM[s])
                        if s - 1 in XT_SLOT:
                            a_evacuate(t, XT_SLOT[s - 1])
                        if s - 1 in V_SLOT:
                            v_evacuate(t, (it.p + 1) % PER_SEQ, V_SLOT[s - 1])
                    if s - 2 in QK_SLOT:
                        hg = QK_SLOT[s - 2]
                        if it.has_now if hg == 3 else it.has_next:
                            qk_hi(it.t if hg == 3 else it.t + 1, hg)
                    if it.has_prev:
                        t = it.t - 1
                        if s - 1 in WO_SLOT:
                            y_evacuate(t, WO_SLOT[s - 1])
                        if s in Y_NORM:
                            y_norm(t, Y_NORM[s])
                        if s in B_STATS:
                            b_stats(t, B_STATS[s])
                        if s in B_NORM:
                            b_norm(t, B_NORM[s])
                        if s - 1 in X2_SLOT:
                            b_evacuate(t, X2_SLOT[s - 1])
                        if s == Z_SLOT + 1:
                            z_rest(t)
                        if s == Z_SLOT + 2:
                            z_last(t)
                        if s - 2 in FF1_SLOT:
                            square_lo(t, FF1_SLOT[s - 2])
                        if s - 1 in FF2_SLOT and FF2_SLOT[s - 1] % 2:
                            c_evacuate(t, FF2_SLOT[s - 1] // 2)
                        if s - 2 in FF2_SLOT and FF2_SLOT[s - 2] % 2:
                            c_norm(t, FF2_SLOT[s - 2] // 2)

            run_iterations(v, body)

        @block.gpsimd
        def _(g):
            def rstd(k, row, n):
                g.wait_ge(M[k + "_ve"], n + 1)
                g.tensor_tensor(lnrs[:, row, 0:1], lnve[:, row, :], W["nhalf"][:], ALU.pow).then_inc(M[k + "_rs"], 1)

            def a_lo(t, i):
                n = t * TILES + i
                g.wait_ge(M["a_xh"], n + 1)
                need(g, M["A_full"], t * NA + i if i else (t - 1) * NA + TILES)
                g.tensor_tensor(xl[:], xn[:], xh[:], ALU.subtract).then_inc(M["a_xl"], 1)

            def qk_lo(t, hg):
                g.wait_ge(M["qk_hi_done"], t * NGROUP + hg + 1)
                need(g, M["S_full"], (t - 1) * SLOTS + (hg + 1) * TILES * GROUP)
                g.tensor_tensor(qkp[:, 1], qk32[:], qkp[:, 0], ALU.subtract).then_inc(M["qk_lo_done"], 1)

            def out_lo(t, hg):
                g.wait_ge(M["OT_hi"], t * NGROUP + hg + 1)
                g.tensor_tensor(OT[:, 1, hg, :], o32[:], OT[:, 0, hg, :], ALU.subtract).then_inc(M["OT_lo"], 1)

            def first_residual(t, i):
                n = t * TILES + i
                g.wait_ge(M["y_n"], n + 1)
                g.wait_ge(M[f"xr_in{i}"], (t + 1) * 16)
                need(g, M["c_out"], (t - 1) * TILES + i + 1)
                g.tensor_tensor(x1[:, i, :], yb[:], xr[:, i, :], ALU.add).then_inc(M["x1_done"], 1)

            def b_lo(t, i):
                n = t * TILES + i
                g.wait_ge(M["b_xh"], n + 1)
                need(g, M["C_full"], t * NC + 2 + i if i else (t - 1) * NC + 2 + TILES)
                g.tensor_tensor(x2l[:], x2n[:], x2h[:], ALU.subtract).then_inc(M["b_xl"], 1)

            def square(t, m):
                g.wait_ge(M[f"F_free{m % 2}"], t * NF + m // 2 + 1)
                need(g, M["r2_lo"], t * (KH // 2) + m)
                g.tensor_tensor(sq32[:], r32[:], r32[:], ALU.mult).then_inc(M["r2_sq"], 1)

            def second_residual(t, i):
                n = t * TILES + i
                g.wait_ge(M["c_n"], n + 1)
                g.tensor_tensor(yc[:, i, :], yc[:, i, :], x1[:, i, :], ALU.add).then_inc(M["c_out"], 1)

            def body(it):
                for s in range(SLOTS):
                    ok, t, p, j = lagged(it, s, LAG_OT)
                    if ok and j % (TILES * GROUP) == TILES * GROUP - 1:
                        out_lo(t, block_of(j)[0])
                    if it.has_next:
                        t = it.t + 1
                        if s in A_STATS:
                            rstd("a", 0, t * TILES + A_STATS[s])
                        if s in A_NORM:
                            a_lo(t, A_NORM[s])
                    if s - 2 in QK_SLOT:
                        hg = QK_SLOT[s - 2]
                        if it.has_now if hg == 3 else it.has_next:
                            qk_lo(it.t if hg == 3 else it.t + 1, hg)
                    if it.has_prev:
                        t = it.t - 1
                        if s - 1 in WO_SLOT:
                            rstd("y", 1, t * TILES + WO_SLOT[s - 1])
                        if s in Y_NORM:
                            first_residual(t, Y_NORM[s])
                        if s in B_STATS:
                            rstd("b", 2, t * TILES + B_STATS[s])
                        if s in B_NORM:
                            b_lo(t, B_NORM[s])
                        if s - 1 in FF1_SLOT:
                            square(t, FF1_SLOT[s - 1])
                        if s - 1 in FF2_SLOT and FF2_SLOT[s - 1] % 2:
                            rstd("c", 3, t * TILES + FF2_SLOT[s - 1] // 2)
                        if s - 2 in FF2_SLOT and FF2_SLOT[s - 2] % 2:
                            second_residual(t, FF2_SLOT[s - 2] // 2)

            run_iterations(g, body)


def build(nc, A, out):
    with ExitStack() as ctx:
        def sb(name, shape, dt):
            return ctx.enter_context(nc.sbuf_tensor(name, shape, dt))

        W = {
            "w": sb("w_attn", [P, 4, 2, KD, D], F16),
            "t1": sb("t1", [P, KD, HIDDEN], F16),
            "t2": sb("t2", [P, KH, D], F16),
            "u": sb("u_T", [LR, HIDDEN], BF16),
            "v": sb("v_T", [P, 2, KD, LR], F16),
            "bo": sb("bo_rows", [P, D], F32), "bv": sb("bv_rows", [P, D], F32),
            "s2": sb("s2_rows", [P, D], F32),
            "mask": sb("mask", [P, WIN], F32),
            "idf": sb("idf", [P, P], F32), "idh": sb("idh", [P, P], F16), "idb": sb("idb", [P, P], BF16),
            "nhalf": sb("nhalf", [P, 1], F32), "zsel": sb("zsel", [P, 2], F32),
            "c": sb("scales", [P, 12], F32), "c1": sb("c1", [P, KH], F32),
            "bqs": sb("bqs", [P, 2, KD], F32),
            "consts": ctx.enter_context(nc.semaphore("consts_ready")),
        }
        prepare(nc, A, W)
        steps(nc, A, W, out)



def kernel(**inputs):
    import numpy as np
    import concourse.bacc as bacc
    from concourse.bass_utils import run_bass_kernel_spmd

    nc = bacc.Bacc("TRN2", target_bir_lowering=False, num_devices=1)
    arrays, A = {}, {}
    for name, a in inputs.items():
        short = name.replace("L0_attn_", "").replace("L0_ffn_", "")
        a = np.ascontiguousarray(a)
        if short == "x":
            a = a.reshape(BATCH * SEQ, D)
        if short == "gate":
            a = a.reshape(1)
        arrays[f"in_{short}"] = a
        A[short] = nc.dram_tensor(f"in_{short}", a.shape, mybir.dt.from_np(a.dtype), kind="ExternalInput").ap()
    out = nc.dram_tensor("out_0", (BATCH * SEQ, D), F32, kind="ExternalOutput").ap()
    build(nc, A, out)
    r = run_bass_kernel_spmd(nc, [arrays], core_ids=[0])
    return r.results[0]["out_0"].reshape(BATCH, SEQ, D)
```

```python
from contextlib import ExitStack

import concourse.bass as bass
from concourse import mybir

P = 128
BATCH, SEQ, D = 8, 1024, 512
HEADS, HD = 16, 32
HIDDEN, RANK = 2048, 16
WINDOW = 256
STEP = 256
TILES = STEP // P
PER_SEQ = SEQ // STEP
NSTEP = BATCH * PER_SEQ
KD = D // P
KH = HIDDEN // P
GROUP = P // HD
NGROUP = HEADS // GROUP
SLOTS = NGROUP * TILES * GROUP
NKC = WINDOW // P + 1
WIN = NKC * P
RING = 2 * STEP
ST = 3 * HD
LR = 6 * RANK
EPS = 1e-5
XS = 2.0 ** 11
NEG = -1e38

F32, F16, BF16, U32 = mybir.dt.float32, mybir.dt.float16, mybir.dt.bfloat16, mybir.dt.uint32
ALU, ACT, AX = mybir.AluOpType, mybir.ActivationFunctionType, mybir.AxisListType
RADD, RMAX = bass.bass_isa.ReduceOp.add, bass.bass_isa.ReduceOp.max

XT_SLOT = {3: 0, 6: 1}
V_SLOT = {7: (0, 0), 8: (0, 1), 11: (1, 0), 13: (1, 1)}
QK_SLOT = {14: (0, 0), 15: (0, 1), 17: (1, 0), 20: (1, 1), 27: (2, 0), 29: (2, 1), 32: (3, 0), 33: (3, 1)}
X_SLOT = {21: 0}
XR_SLOT = {16: 0}
WO_SLOT = {5: (0, 0), 6: (0, 1), 9: (1, 0), 10: (1, 1)}
X2_SLOT = {12: 0, 14: 1}
Z_SLOT = {16: 0}
FF1_SLOT = {18: 0, 19: 1, 20: 2, 21: 3, 22: 4, 23: 5, 24: 6, 25: 7}
FF2_PIECES = 4
FF2_SLOT = {24: (0, 0), 26: (0, 1), 27: (0, 2), 28: (0, 3), 30: (1, 0), 33: (1, 1), 34: (1, 2), 36: (1, 3)}
A_STATS, A_NORM = {0: 0, 2: 1}, {1: 0, 4: 1}
Y_NORM, B_STATS, B_NORM = {8: 0, 11: 1}, {9: 0, 12: 1}, {10: 0, 12: 1}
LAG_T, LAG_PV = 2, 3
LAG_RB, LAG_O, LAG_OT = 1, 4, 5


def need(eng, sem, value):
    if isinstance(value, int) and value <= 0:
        return
    eng.wait_ge(sem, value)


def settled_wait(eng, consts, sem, value):
    if not isinstance(value, int):
        value = eng.to_reg(value)
    eng.wait_ge(consts, 1)
    eng.wait_ge(sem, value)


class Iteration:

    def __init__(self, t, p):
        self.t, self.p = t, p

    def has(self, k):
        return not isinstance(self.t, int) or 0 <= self.t + k < NSTEP

    def step(self, k):
        return self.t + k, (self.p + k) % PER_SEQ


def run_iterations(eng, body):
    for t in range(-1, 2):
        body(Iteration(t, t % PER_SEQ))
    n = NSTEP // PER_SEQ - 1
    with eng.Fori(0, n, 1) as i:
        for q in range(PER_SEQ):
            body(Iteration(i * PER_SEQ + (2 + q), (2 + q) % PER_SEQ))
    for t in range(2 + n * PER_SEQ, NSTEP + 2):
        body(Iteration(t, t % PER_SEQ))


def due(it, table, slot, lag, base):
    for back in range(3):
        entry = table.get(slot - lag + back * SLOTS)
        if entry is not None and it.has(base - back):
            yield (*it.step(base - back), entry)


def lagged(it, slot, lag):
    j = slot - lag
    back = 0 if j >= 0 else 1
    return (it.has(-back), *it.step(-back), j + back * SLOTS)


def block_of(j):
    return j // (TILES * GROUP), j // GROUP % TILES, j % GROUP


def key_chunks(p, qc):
    c = p * TILES + qc
    return [(i, c - NKC + 1 + i) for i in range(NKC) if c - NKC + 1 + i >= 0]


def prepare(nc, A, W):
    with ExitStack() as ctx:
        def sb(name, shape, dt):
            return ctx.enter_context(nc.sbuf_tensor(name, shape, dt))

        def sem(name):
            return ctx.enter_context(nc.semaphore(name))

        stage = [sb(f"stage{i}", [P, 4 * D], F32) for i in range(3)]
        s_hi = [sb(f"s_hi{i}", [P, 4 * D], F16) for i in range(2)]
        s_lo = [sb(f"s_lo{i}", [P, 4 * D], F16) for i in range(2)]
        junk = [sb(f"junk{i}", [P, 4 * D], F16) for i in range(2)]
        u_in = sb("u_in", [P, KH, RANK], F32)
        u_sc = sb("u_sc", [P, KH, RANK], F32)
        u_r = sb("u_r", [P, KH, RANK], F32)
        u_part = sb("u_part", [P, 3, KH, RANK], BF16)
        u_stack = sb("u_stack", [P, KH, LR], BF16)
        v_in = sb("v_in", [RANK, D], F32)
        fbT = sb("fbT", [RANK, RANK], F32)
        fb6 = sb("fb6", [RANK, LR], F32)
        vp = sb("vp", [P, KD, LR], F32)
        vsq = sb("vsq", [P, KD, RANK], F32)
        usq = sb("usq", [P, KH], F32)
        gate = sb("gate", [P, 1], F32)
        bqk = sb("bqk", [P, 2, KD], F32)
        red = sb("red", [P, 16], F32)
        redA = sb("redA", [P, 16], F32)
        vss = sb("vss", [P, 2], F32)
        bnd = sb("bnd", [P, 9], F32)
        p2 = sb("p2", [P, 9], F32)
        inv = sb("inv", [P, 9], F32)
        pow_in = sb("pow_in", [P, 2], F32)
        pow_ex = sb("pow_ex", [P, 2], F32)
        pow_out = sb("pow_out", [P, 2], F32)
        g23 = sb("g23", [P, 2], F32)
        s1 = sb("s1", [P, KH], F32)
        s2 = sb("s2", [P, KD], F32)
        h1 = sb("h1", [P, 2, KH], F32)
        h2 = sb("h2", [P, 2, KD], F32)
        fac = sb("fac", [P, KH], F32)
        s2c = sb("s2c", [P, KD], F32)
        sW = sb("sW", [P, 4], F32)
        ps = [ctx.enter_context(nc.psum_tensor(f"pp{i}", [P, 512], F32)) for i in range(4)]

        loaded = [sem(f"loaded{i}") for i in range(3)]
        s_small = sem("small_loaded")
        s_pool = sem("pool_ready")
        dch = sem("dve_step")
        s_stage_free = sem("stage_free")
        s_hi_done = sem("hi_done")
        s_act_hi = sem("weights_hi")
        s_scales = sem("weight_scales_ready")
        s_sums = sem("abs_sums")
        s_bounds = sem("bound_inputs")
        s_pt = sem("prep_transposed")
        s_ev = {"dve": sem("prep_evacuated_dve"), "act": sem("prep_evacuated_act")}
        s_red = sem("red_ready")
        s_red_all = sem("red_all")
        block = ctx.enter_context(nc.Block())

        src = ([w.rearrange("(c p) i -> p c i", p=P) for w in (A["Wq"], A["Wk"], A["Wv"], A["Wo"])]
               + [A["w_fc"].rearrange("(m p) i -> p m i", p=P)[:, 4 * n:4 * n + 4, :] for n in range(4)]
               + [A["w_proj"].rearrange("(c p) h -> p c h", p=P)[:, n:n + 1, :] for n in range(4)])
        order = [0, 1, 2, 3] + [4, 5, 6, 7] + [8, 9, 10, 11] + [0, 1, 2, 3]
        NPIECE = len(order)

        def piece(n):
            return stage[n % 3][:, :]

        @block.sync
        def _(sp):
            sp.dma_start(u_in[:], A["u"].rearrange("(m p) r -> p m r", p=P)).then_inc(s_small, 16)
            sp.dma_start(v_in[:], A["v"]).then_inc(s_small, 16)
            with nc.allow_non_contiguous_dma(reason="256 words"):
                sp.dma_start(fbT[:], A["fast_b"].rearrange("a r -> r a")).then_inc(s_small, 16)
                sp.dma_start(bqk[:, 0, :], A["bq"].rearrange("(c p) -> p c", p=P)).then_inc(s_small, 16)
                sp.dma_start(bqk[:, 1, :], A["bk"].rearrange("(c p) -> p c", p=P)).then_inc(s_small, 16)
            sp.dma_start(gate[:], A["gate"].rearrange("(a b) -> a b", a=1).to_broadcast([P, 1])).then_inc(s_small, 16)
            sp.dma_start(W["bv"][:], A["bv"].rearrange("(a d) -> a d", a=1).to_broadcast([P, D])).then_inc(s_small, 16)
            sp.dma_start(W["bo"][:], A["bo"].rearrange("(a d) -> a d", a=1).to_broadcast([P, D])).then_inc(s_small, 16)
            for n in range(NPIECE):
                if n >= 3:
                    m = n - 3
                    sp.wait_ge(*((s_stage_free, m + 1) if m < 4 else (s_hi_done, m - 3)))
                a = src[order[n]]
                d = piece(n).rearrange("p (c i) -> p c i", c=a.shape[1])
                sp.dma_start(d, a).then_inc(loaded[n % 3], 16)

        @block.gpsimd
        def _(g):
            g.memset(W["idf"][:], 0.0)
            g.memset(W["mask"][:], 0.0)
            g.memset(W["nhalf"][:], -0.5).then_inc(W["consts"], 1)
            g.memset(W["zsel"][:], -1.0)
            g.memset(pow_ex[:], 0.5).then_inc(s_pool, 1)
            g.wait_ge(s_pool, 1)
            g.affine_select(out=W["idf"][:], in_=W["idf"][:], compare_op=ALU.not_equal, fill=1.0, base=0,
                            pattern=[[-1, P]], channel_multiplier=1)
            m0, m2 = W["mask"][:, 0:P], W["mask"][:, WIN - P:WIN]
            g.affine_select(out=m0, in_=m0, compare_op=ALU.is_gt, fill=NEG, base=0,
                            pattern=[[1, P]], channel_multiplier=-1)
            g.affine_select(out=m2, in_=m2, compare_op=ALU.is_ge, fill=NEG, base=0,
                            pattern=[[-1, P]], channel_multiplier=1)
            for col, group in ((0, 3), (1, 5)):
                zs = W["zsel"][:, col:col + 1]
                last = g.affine_select(out=zs, in_=zs, compare_op=ALU.is_ge, fill=0.0, base=-group * RANK,
                                       pattern=[[0, 1]], channel_multiplier=1)
            last.then_inc(s_pool, 1)
            g.wait_ge(s_pool, 2)
            g.tensor_copy(W["idh"][:], W["idf"][:])
            g.tensor_copy(W["idb"][:], W["idf"][:]).then_inc(s_pool, 1)
            g.wait_ge(s_red, 1)
            g.partition_all_reduce(redA[:, 0:9], red[:, 0:9], P, RMAX).then_inc(s_red_all, 1)
            g.wait_ge(s_red, 2)
            g.partition_all_reduce(vss[:, 1:2], vss[:, 0:1], P, RADD).then_inc(s_red_all, 1)
            g.wait_ge(s_bounds, 1)
            g.tensor_tensor(pow_out[:], pow_in[:], pow_ex[:], ALU.pow).then_inc(s_red_all, 1)

        jobs = (["vp"] + [("t1", n, h) for n in range(4) for h in range(2)]
                + [("t2", n, h) for n in range(4) for h in range(2)] + ["s2"]
                + [("u", h) for h in range(2)] + [("w", n, c) for n in range(4) for c in range(4)])

        def owner(n):
            return "act" if jobs[n][0] in ("t1", "t2") or (jobs[n][0] == "w" and n % 2) else "dve"

        def rank(n):
            return sum(owner(k) == owner(n) for k in range(n + 1))

        def evacuate(eng, who, n0, n1):
            for n in range(n0, n1):
                if owner(n) != who:
                    continue
                job, b = jobs[n], ps[n % 4]
                bh = b[:, :].bitcast(F16)
                if job == "vp":
                    dst, a = vp[:].rearrange("p k c -> p (k c)"), b[:, 0:KD * LR]
                elif job == "s2":
                    dst, a = W["s2"][:], b[:, :]
                elif job[0] == "t1":
                    m = 4 * job[1] + 2 * job[2]
                    dst, a = W["t1"][:, :, m * P:(m + 2) * P], bh.rearrange("p (k c) -> p k c", k=KD)
                elif job[0] == "t2":
                    _, c, h = job
                    dst = W["t2"][:, 8 * h:8 * h + 8, c * P:(c + 1) * P]
                    a = bh.rearrange("p (m c) -> p m c", m=8)
                elif job[0] == "u":
                    h = job[1]
                    dst, a = W["u"][:, 8 * h * P:(8 * h + 8) * P], b[0:LR, :].bitcast(BF16)
                else:
                    _, w, c = job
                    dst = W["w"][:, w].rearrange("p a k o -> p (a k) o")[:, :, c * P:(c + 1) * P]
                    a = bh.rearrange("p (g c) -> p g c", g=2 * KD)
                eng.wait_ge(s_pt, n + 1)
                ins = eng.tensor_copy(dst, a) if who == "dve" else eng.activation(dst, a, ACT.Copy)
                ins.then_inc(s_ev[who], 1)

        @block.tensor
        def _(pe):
            pe.wait_ge(s_pool, 3)
            for n, job in enumerate(jobs):
                if n >= 4:
                    pe.wait_ge(s_ev[owner(n - 4)], rank(n - 4))
                b = ps[n % 4]
                bh = b[:, :].bitcast(F16)
                if job == "vp":
                    pe.wait_ge(dch, 1)
                    for k in range(KD):
                        last = pe.matmul(b[:, k * LR:(k + 1) * LR], v_in[:, k * P:(k + 1) * P], fb6[:],
                                         start=True, stop=True)
                elif job == "s2":
                    pe.wait_ge(s_red, 3)
                    for c in range(KD):
                        last = pe.transpose(b[:, c * P:(c + 1) * P], s2c[:, c:c + 1].to_broadcast([P, P]),
                                            W["idf"][:])
                elif job[0] == "t1":
                    _, n4, h = job
                    pe.wait_ge(s_hi_done, n4 + 1)
                    for k in range(KD):
                        for mm in range(2):
                            m = 2 * h + mm
                            last = pe.transpose(bh[:, k * 256 + mm * P:k * 256 + mm * P + P],
                                                s_hi[n4 % 2][:, m * D + k * P:m * D + k * P + P], W["idh"][:])
                elif job[0] == "t2":
                    _, c, h = job
                    pe.wait_ge(s_hi_done, 4 + c + 1)
                    for m in range(8):
                        last = pe.transpose(bh[:, m * P:m * P + P],
                                            s_hi[c % 2][:, (8 * h + m) * P:(8 * h + m + 1) * P], W["idh"][:])
                elif job[0] == "u":
                    h = job[1]
                    pe.wait_ge(s_red, 4)
                    bb = b[:, :].bitcast(BF16)
                    for m in range(8):
                        last = pe.transpose(bb[0:LR, m * P:m * P + P], u_stack[:, 8 * h + m, :], W["idb"][:])
                else:
                    _, w, c = job
                    pe.wait_ge(s_hi_done, 8 + w + 1)
                    for part, t in enumerate((s_hi, s_lo)):
                        for k in range(KD):
                            last = pe.transpose(bh[:, (part * KD + k) * P:(part * KD + k + 1) * P],
                                                t[w % 2][:, c * D + k * P:c * D + k * P + P], W["idh"][:])
                last.then_inc(s_pt, 1)

        @block.scalar
        def _(act):
            for m in range(8):
                n = 4 + m
                s, w = (s1, 4) if m < 4 else (s2, 1)
                c0 = w * (m % 4)
                act.wait_ge(loaded[n % 3], 16 * (n // 3 + 1))
                if m >= 2:
                    act.wait_ge(s_sums, m - 1)
                for c in range(w):
                    cols = slice(c * 4 * D // w, (c + 1) * 4 * D // w)
                    ins = act.activation(junk[m % 2][:, cols], piece(n)[:, cols], ACT.Abs,
                                         accum_out=s[:, c0 + c:c0 + c + 1])
                ins.then_inc(s_sums, 1)
                if m >= 2:
                    evacuate(act, "act", 2 * m - 3, 2 * m - 1)
            evacuate(act, "act", 13, 17)
            act.wait_ge(s_scales, 1)
            for w in range(4):
                n = 12 + w
                act.wait_ge(loaded[n % 3], 16 * (n // 3 + 1))
                if w >= 2:
                    act.wait_ge(s_pt, len(jobs) - 16 + 4 * (w - 1))
                act.activation(s_hi[w % 2][:], piece(n), ACT.Identity, scale=sW[:, w:w + 1]).then_inc(s_act_hi, 1)
                if w >= 1:
                    evacuate(act, "act", 16 + 4 * w, 20 + 4 * w)
            evacuate(act, "act", 32, 36)

        @block.vector
        def _(v):
            count = {}

            def then(ins, sem=dch):
                count[sem.name] = count.get(sem.name, 0) + 1
                ins.then_inc(sem, 1)
                v.wait_ge(sem, count[sem.name])

            v.wait_ge(s_small, 16 * 8)
            then(v.tensor_copy(fb6[:].rearrange("p (g r) -> p g r", g=6),
                               fbT[:].rearrange("p (g r) -> p g r", g=1).to_broadcast([RANK, 6, RANK])))
            then(v.tensor_tensor(u_sc[:], u_in[:], u_in[:], ALU.mult))
            then(v.tensor_reduce(usq[:], u_sc[:], AX.X, ALU.add))
            v.tensor_reduce(red[:, 8:9], usq[:], AX.X, ALU.max)
            v.tensor_reduce(red[:, 4:6], bqk[:], AX.X, ALU.max, apply_absolute_value=True)
            v.tensor_reduce(red[:, 6:7], W["bv"][:], AX.X, ALU.max, apply_absolute_value=True)
            for n in range(12):
                if n < 4:
                    v.wait_ge(loaded[n % 3], 16 * (n // 3 + 1))
                    v.tensor_reduce(red[:, n:n + 1], piece(n), AX.X, ALU.max,
                                    apply_absolute_value=True).then_inc(s_stage_free, 1)
                    continue
                m = n - 4
                s, h, w = (s1, h1, 4) if m < 4 else (s2, h2, 1)
                c0 = w * (m % 4)
                pc = piece(n).rearrange("p (c i) -> p c i", c=w)
                v.wait_ge(s_sums, m + 1)
                then(v.tensor_scalar(s[:, c0:c0 + w], s[:, c0:c0 + w], w / (4.0 * D), EPS, ALU.mult, ALU.max))
                v.tensor_scalar(h[:, 0, c0:c0 + w], s[:, c0:c0 + w], -0.5, None, ALU.mult)
                then(v.tensor_scalar(h[:, 1, c0:c0 + w], s[:, c0:c0 + w], 0.5, None, ALU.mult))
                if m == 1:
                    evacuate(v, "dve", 0, 1)
                if m >= 2:
                    v.wait_ge(s_pt, 2 * m - 1)
                o = s_hi[m % 2][:].rearrange("p (c i) -> p c i", c=w)
                below = s_lo[m % 2][:].rearrange("p (c i) -> p c i", c=w)
                for c in range(w):
                    last = v.tensor_scalar(below[:, c], pc[:, c], h[:, 0, c0 + c:c0 + c + 1], None, ALU.is_lt)
                then(last)
                for c in range(w):
                    last = v.scalar_tensor_tensor(o[:, c], pc[:, c], h[:, 1, c0 + c:c0 + c + 1], below[:, c],
                                                  ALU.is_gt, ALU.subtract)
                then(last, s_hi_done)
                if m == 3:
                    then(v.tensor_reduce(red[:, 7:8], s1[:], AX.X, ALU.max), s_red)
            v.wait_ge(s_ev["dve"], 1)
            then(v.tensor_tensor(vsq[:], vp[:, :, 0:RANK], vp[:, :, 0:RANK], ALU.mult))
            then(v.tensor_reduce(vss[:, 0:1], vsq[:], AX.XY, ALU.add), s_red)
            v.wait_ge(s_red_all, 2)
            v.tensor_tensor(pow_in[:, 0:1], redA[:, 8:9], vss[:, 1:2], ALU.mult)
            then(v.tensor_copy(pow_in[:, 1:2], vss[:, 1:2]), s_bounds)
            v.tensor_copy(bnd[:, 0:4], redA[:, 0:4])
            v.scalar_tensor_tensor(bnd[:, 4:7], redA[:, 0:3], 1.01 * D, redA[:, 4:7], ALU.mult, ALU.add)
            then(v.scalar_tensor_tensor(g23[:, 0:1], gate[:], -1.0, gate[:], ALU.mult, ALU.max))
            v.wait_ge(s_red_all, 3)
            v.tensor_scalar(bnd[:, 7:8], pow_out[:, 1:2], 1.01, None, ALU.mult)
            then(v.scalar_tensor_tensor(g23[:, 1:2], g23[:, 0:1], 23.0, pow_out[:, 0:1], ALU.mult, ALU.mult))
            then(v.scalar_tensor_tensor(bnd[:, 8:9], redA[:, 7:8], 1.01 * D, g23[:, 1:2], ALU.mult, ALU.add))
            then(v.tensor_scalar(bnd[:], bnd[:], 1e-20, None, ALU.max))
            then(v.tensor_scalar(p2[:].bitcast(U32), bnd[:].bitcast(U32), 0x7F800000, None, ALU.bitwise_and))
            then(v.reciprocal(inv[:], p2[:]))
            v.tensor_scalar(sW[:], inv[:, 0:4], 2.0 ** 14, None, ALU.mult).then_inc(s_scales, 1)
            c = W["c"]
            v.tensor_tensor(c[:, 0:3], inv[:, 4:7], p2[:, 0:3], ALU.mult)
            v.tensor_tensor(c[:, 3:4], p2[:, 4:5], p2[:, 5:6], ALU.mult)
            v.tensor_scalar(c[:, 5:8], inv[:, 4:7], 2.0 ** 14, None, ALU.mult)
            v.tensor_scalar(c[:, 8:9], inv[:, 8:9], 2.0 ** 6 / XS, None, ALU.mult)
            v.tensor_tensor(c[:, 9:10], p2[:, 8:9], p2[:, 8:9], ALU.mult)
            v.tensor_scalar(c[:, 10:11], inv[:, 7:8], 2.0 ** 14, None, ALU.mult)
            v.tensor_scalar(c[:, 11:12], p2[:, 7:8], 2.0 ** -14, gate[:, 0:1], ALU.mult, ALU.mult)
            v.reciprocal(fac[:], s1[:])
            then(v.tensor_tensor(c[:, 4:5], p2[:, 6:7], p2[:, 3:4], ALU.mult))
            v.tensor_scalar(c[:, 0:3], c[:, 0:3], 1.0 / XS, None, ALU.mult)
            v.tensor_scalar(c[:, 3:4], c[:, 3:4], -(float(HD) ** -0.5) * 2.0 ** -28, None, ALU.mult)
            v.tensor_scalar(c[:, 4:5], c[:, 4:5], 2.0 ** -28, None, ALU.mult)
            v.tensor_scalar(W["bqs"][:, 0, :], bqk[:, 0, :], c[:, 5:6], None, ALU.mult)
            v.tensor_scalar(W["bqs"][:, 1, :], bqk[:, 1, :], c[:, 6:7], None, ALU.mult)
            v.tensor_scalar(W["bv"][:], W["bv"][:], c[:, 7:8], None, ALU.mult)
            v.tensor_scalar(W["c1"][:], s1[:], c[:, 8:9], None, ALU.mult)
            v.tensor_scalar(fac[:], fac[:], c[:, 11:12], None, ALU.mult)
            then(v.tensor_scalar(vp[:], vp[:], c[:, 10:11], None, ALU.mult))
            v.tensor_scalar(s2c[:], s2[:], c[:, 9:10], 2.0 ** -12, ALU.mult, ALU.mult).then_inc(s_red, 1)
            then(v.tensor_copy(W["v"][:, 0], vp[:]))
            v.tensor_tensor(W["v"][:, 1], vp[:], W["v"][:, 0], ALU.subtract)
            then(v.tensor_tensor(u_sc[:], u_in[:],
                                 fac[:].rearrange("p (m o) -> p m o", o=1).to_broadcast([P, KH, RANK]), ALU.mult))
            then(v.tensor_copy(u_part[:, 0], u_sc[:]))
            then(v.tensor_tensor(u_r[:], u_sc[:], u_part[:, 0], ALU.subtract))
            then(v.tensor_copy(u_part[:, 1], u_r[:]))
            then(v.tensor_tensor(u_part[:, 2], u_r[:], u_part[:, 1], ALU.subtract))
            for g, part in enumerate((0, 1, 2, 0, 1, 0)):
                last = v.tensor_copy(u_stack[:, :, g * RANK:(g + 1) * RANK], u_part[:, part])
            last.then_inc(s_red, 1)
            evacuate(v, "dve", 17, 20)
            for w in range(4):
                n = 12 + w
                v.wait_ge(s_act_hi, w + 1)
                if w >= 2:
                    v.wait_ge(s_pt, 20 + 4 * (w - 1))
                v.scalar_tensor_tensor(s_lo[w % 2][:], piece(n), sW[:, w:w + 1], s_hi[w % 2][:], ALU.mult,
                                       ALU.subtract).then_inc(s_hi_done, 1)
                if w >= 1:
                    evacuate(v, "dve", 16 + 4 * w, 20 + 4 * w)
            evacuate(v, "dve", 32, 36)


def steps(nc, A, W, out):
    with ExitStack() as ctx:
        def sb(name, shape, dt):
            return ctx.enter_context(nc.sbuf_tensor(name, shape, dt))

        def bank(name):
            return ctx.enter_context(nc.psum_tensor(name, [P, 512], F32))

        def sem(name):
            return ctx.enter_context(nc.semaphore(name))

        xa = sb("xa", [P, TILES, D], F32)
        xn = sb("xn", [P, D], F32)
        xh, xl = sb("xh", [P, D], F16), sb("xl", [P, D], F16)
        xT = sb("xT", [P, 2, KD, STEP], F16)
        qk32 = sb("qk32", [P, 2, STEP], F32)
        qkp = sb("qkp", [P, 2, 2, 2, STEP], F16)
        QK3 = sb("QK3", [ST, HEADS, 1 + RING // STEP, STEP], F16)
        Q3, K3 = QK3[:, :, 0, :], QK3[:, :, 1:, :].rearrange("p h b n -> p h (b n)")
        V = sb("V", [P, SEQ // P, D], F32)
        NSM, NPT = 4, 8
        Sm = sb("Sm", [P, NSM, WIN], F32)
        nmax = sb("nmax", [P, 8], F32)
        sums = sb("sums", [P, 2, TILES, GROUP], F32)
        PTs = sb("PTs", [P, NPT, WIN], F32)
        rinv = sb("rinv", [P, TILES * GROUP, 1], F32)
        rb = sb("rb", [P, TILES * GROUP, HD], F32)
        Rs = sb("Rs", [P, STEP], F32)
        o32 = sb("o32", [P, STEP], F32)
        OT = sb("OT", [P, 2, NGROUP, STEP], F16)
        xr = sb("xr", [P, TILES, D], F32)
        yb = sb("yb", [P, D], F32)
        x1 = sb("x1", [P, TILES, D], F32)
        x2n = sb("x2n", [P, D], F32)
        x2h, x2l = sb("x2h", [P, D], F16), sb("x2l", [P, D], F16)
        x2T = sb("x2T", [P, 2, KD, STEP], F16)
        z_h, z_m, z6 = (sb(n, [LR, STEP], BF16) for n in ("z_h", "z_m", "z6"))
        z_r = sb("z_r", [LR, STEP], F32)
        r32, sq32 = sb("r32", [P, 2 * STEP], F32), sb("sq32", [P, 2 * STEP], F32)
        r2 = sb("r2", [P, 2, KH, STEP], F16)
        yc = sb("yc", [P, TILES, D], F32)
        lnst = sb("lnst", [P, 4, 6], F32)
        lnmv = sb("lnmv", [P, 4, 2], F32)
        lnve = sb("lnve", [P, 4, 1], F32)
        lnrs = sb("lnrs", [P, 4, 2], F32)

        Sb = [bank("S0"), bank("S1")]
        PTb, Ob = bank("PTb"), bank("Ob")
        Fb = [bank("F0"), bank("F1")]
        Ab, Cb = bank("Ab"), bank("Cb")

        names = """xa_in0 xa_in1 a_st a_mv a_ve a_rs a_xn a_xh a_xl
            A_full A_free  qk_hi_done qk_lo_done stacked0 stacked1 stacked2 stacked3
            S_full S_done S_exp T_full PT_copied_act PT_copied_dve PT_used rinv_done rb_done O_full Rs_done o32_done
            OT_hi OT_lo
            xr_in0 xr_in1 y_done y_st y_mv y_ve y_rs y_n x1_done b_st b_mv b_ve b_rs b_xn b_xh b_xl
            C_full C_free z_hi z_r1 z_mid z_done F_full0 F_full1 F_free0 F_free1 relu_done r2_hi r2_sq r2_lo
            c_y c_st c_mv c_ve c_rs c_n c_out stored0 stored1""".split()
        M = {n: sem(n) for n in names}

        def copied(eng, t, j):
            need(eng, M["PT_copied_dve" if j % 2 else "PT_copied_act"], t * (SLOTS // 2) + j // 2 + 1)

        NA = 8
        NC = 6
        NF = (5, 4)

        def xrow(ap, t, i):
            if isinstance(t, int):
                r0 = t * STEP + i * P
                return ap[r0:r0 + P, :]
            return ap[bass.ds(t * STEP + i * P, P), :]

        block = ctx.enter_context(nc.Block())

        @block.sync
        def _(sp):
            def load_x(t, i):
                need(sp, M["a_xn"], (t - 1) * TILES + i + 1)
                sp.dma_start(xa[:, i, :], xrow(A["x"], t, i)).then_inc(M[f"xa_in{i}"], 16)

            def stack(t, p, hg):
                ring = 1 + p % (RING // STEP)
                sp.wait_ge(M["qk_hi_done"], t * NGROUP + hg + 1)
                sp.wait_ge(M["qk_lo_done"], t * NGROUP + hg + 1)
                for r in range(GROUP):
                    parts = qkp[r * HD:(r + 1) * HD, hg % 2].rearrange("p w a n -> p (w a) n")
                    for term, (qpart, kpart) in enumerate(((0, 0), (0, 1), (1, 0))):
                        kplace = 2 + kpart
                        sp.dma_start(QK3[term * HD:(term + 1) * HD, hg * GROUP + r, 0:ring + 1:ring],
                                     parts[:, qpart:kplace + 1:kplace - qpart]).then_inc(M[f"stacked{hg}"], 16)

            def body(it):
                for s in range(SLOTS):
                    for t, p, _ in due(it, X_SLOT, s, 0, 2):
                        for i in range(TILES):
                            load_x(t, i)
                    for t, p, _ in due(it, XR_SLOT, s, 0, 0):
                        for i in range(TILES):
                            need(sp, M["x1_done"], (t - 1) * TILES + i + 1)
                            sp.dma_start(xr[:, i, :], xrow(A["x"], t, i)).then_inc(M[f"xr_in{i}"], 16)
                    for t, p, (hg, w) in due(it, QK_SLOT, s, 2, 1):
                        if w == 1:
                            stack(t, p, hg)
                    for t, p, (i, piece) in due(it, FF2_SLOT, s, 3, -1):
                        if piece == FF2_PIECES - 1:
                            sp.wait_ge(M["c_out"], t * TILES + i + 1)
                            sp.dma_start(xrow(out, t, i), yc[:, i, :]).then_inc(M[f"stored{i}"], 16)

            for i in range(TILES):
                load_x(0, i)
            run_iterations(sp, body)
            for i in range(TILES):
                sp.wait_ge(M[f"stored{i}"], 16 * NSTEP)

        @block.tensor
        def _(pe):
            def scores(t, p, j):
                hg, qc, r = block_of(j)
                h = hg * GROUP + r
                if qc == 0 and r == 0:
                    pe.wait_ge(M[f"stacked{hg}"], (t + 1) * 3 * GROUP * 16)
                need(pe, M["S_done"], t * SLOTS + j - 1)
                kc = key_chunks(p, qc)
                runs = []
                for place, c in kc:
                    if runs and (c % (RING // P)) == runs[-1][1] + runs[-1][2]:
                        runs[-1][2] += 1
                    else:
                        runs.append([place, c % (RING // P), 1])
                for place, slot, n in runs:
                    mm = pe.matmul(Sb[j % 2][:, place * P:(place + n) * P], Q3[:, h, qc * P:(qc + 1) * P],
                                   K3[:, h, slot * P:(slot + n) * P], start=True, stop=True,
                                   skip_group_check=True)
                mm.then_inc(M["S_full"], 1)

            def transposes(t, p, j):
                hg, qc, r = block_of(j)
                pe.wait_ge(M["S_exp"], t * SLOTS + j + 1)
                copied(pe, t, j - 1)
                for place, _ in key_chunks(p, qc):
                    mm = pe.transpose(PTb[:, place * P:(place + 1) * P],
                                      Sm[:, j % NSM, place * P:(place + 1) * P], W["idf"][:])
                mm.then_inc(M["T_full"], 1)

            def weighted_values(t, p, g):
                hg, qc = g // TILES, g % TILES
                copied(pe, t, GROUP * g + GROUP - 1)
                copied(pe, t, GROUP * g + GROUP - 2)
                if qc == 0:
                    need(pe, M["o32_done"], t * NGROUP + hg)
                pe.wait_ge(M["A_free"], t * NA + 2 + qc + 1)
                kc = key_chunks(p, qc)
                for n, (place, c) in enumerate(kc):
                    for r in range(GROUP):
                        j = g * GROUP + r
                        mm = pe.matmul(Ob[r * HD:(r + 1) * HD, qc * P:(qc + 1) * P],
                                       V[:, c, (hg * GROUP + r) * HD:(hg * GROUP + r + 1) * HD],
                                       PTs[:, j % NPT, place * P:(place + 1) * P],
                                       start=(n == 0), stop=(n == len(kc) - 1), skip_group_check=True)
                mm.then_inc(M["PT_used"], 1)

            def reciprocal_rows(t, hg):
                pe.wait_ge(M["rb_done"], t * NGROUP + hg + 1)
                for qc in range(TILES):
                    mm = pe.transpose(Ob[:, STEP + qc * P:STEP + (qc + 1) * P],
                                      rb[:, qc * GROUP:(qc + 1) * GROUP].rearrange("p r d -> p (r d)"),
                                      W["idf"][:])
                mm.then_inc(M["O_full"], 1)

            def product3(outp, a, b):
                n = 0
                for pa, pb in ((0, 0), (0, 1), (1, 0)):
                    for k in range(KD):
                        mm = pe.matmul(outp, a(pa, k), b(pb, k), start=(n == 0), stop=(n == 3 * KD - 1),
                                       skip_group_check=True)
                        n += 1
                return mm

            def a_transposes(t, i):
                need(pe, M["A_free"], t * NA + i)
                pe.wait_ge(M["a_xh"], t * TILES + i + 1)
                pe.wait_ge(M["a_xl"], t * TILES + i + 1)
                bh = Ab[:, :].bitcast(F16)
                for part, x in enumerate((xh, xl)):
                    for k in range(KD):
                        mm = pe.transpose(bh[:, (part * KD + k) * P:(part * KD + k + 1) * P],
                                          x[:, k * P:(k + 1) * P], W["idh"][:])
                mm.then_inc(M["A_full"], 1)

            def values(t, i, half):
                if half == 0:
                    need(pe, M["A_free"], t * NA + 2 + i)
                cols = slice(half * D // 2, (half + 1) * D // 2)
                mm = product3(Ab[:, cols], lambda a, k: xT[:, a, k, i * P:(i + 1) * P],
                              lambda a, k: W["w"][:, 2, a, k, cols])
                if half == 1:
                    mm.then_inc(M["A_full"], 1)

            def queries_keys(t, hg, w):
                if w == 0:
                    need(pe, M["A_free"], t * NA + 4 + hg)
                mm = product3(Ab[:, w * STEP:(w + 1) * STEP],
                              lambda a, k: W["w"][:, w, a, k, hg * P:(hg + 1) * P],
                              lambda a, k: xT[:, a, k, :])
                if w == 1:
                    mm.then_inc(M["A_full"], 1)

            def out_projection(t, i, half):
                if half == 0:
                    need(pe, M["C_free"], t * (NC - 1) + i)
                pe.wait_ge(M["OT_hi"], (t + 1) * NGROUP)
                pe.wait_ge(M["OT_lo"], (t + 1) * NGROUP)
                cols = slice(half * D // 2, (half + 1) * D // 2)
                mm = product3(Cb[:, cols], lambda a, k: OT[:, a, k, i * P:(i + 1) * P],
                              lambda a, k: W["w"][:, 3, a, k, cols])
                if half == 1:
                    mm.then_inc(M["C_full"], 1)

            def c_transposes(t, i):
                need(pe, M["C_free"], t * (NC - 1) + 2 + i)
                pe.wait_ge(M["b_xh"], t * TILES + i + 1)
                pe.wait_ge(M["b_xl"], t * TILES + i + 1)
                bh = Cb[:, :].bitcast(F16)
                for part, x in enumerate((x2h, x2l)):
                    for k in range(KD):
                        mm = pe.transpose(bh[:, (part * KD + k) * P:(part * KD + k + 1) * P],
                                          x[:, k * P:(k + 1) * P], W["idh"][:])
                mm.then_inc(M["C_full"], 1)

            def low_rank(t):
                pe.wait_ge(M["C_free"], t * (NC - 1) + 2 * TILES)
                mm = product3(Cb[0:LR, 0:STEP], lambda a, k: W["v"][:, a, k, :], lambda a, k: x2T[:, a, k, :])
                mm.then_inc(M["C_full"], 1)

            def hidden(t, m):
                b = m % 2
                need(pe, M[f"F_free{b}"], t * NF[b] + m // 2)
                for half in range(2):
                    mc = 2 * m + half
                    for k in range(KD):
                        for part in range(2):
                            pe.matmul(Fb[b][:, half * STEP:(half + 1) * STEP],
                                      W["t1"][:, k, mc * P:(mc + 1) * P], x2T[:, part, k, :],
                                      start=(half == 0 and k == 0 and part == 0), stop=False,
                                      skip_group_check=True)

            def hidden_low_rank(t, m):
                if m == 0:
                    pe.wait_ge(M["z_done"], t + 1)
                b = m % 2
                for half in range(2):
                    mc = 2 * m + half
                    mm = pe.matmul(Fb[b][:, half * STEP:(half + 1) * STEP], W["u"][:, mc * P:(mc + 1) * P],
                                   z6[:], start=False, stop=True, skip_group_check=True)
                mm.then_inc(M[f"F_full{b}"], 1)

            def ff_out(t, i, q):
                o = Fb[0] if i else Cb
                if q == 0 and i == 0:
                    pe.wait_ge(M["z_r1"], t + 1)
                if q == 0 and i == 1:
                    pe.wait_ge(M["F_free0"], t * NF[0] + 4)
                if i == 0:
                    pairs = t * (KH // 2) + (q + 1) * KH // 2 // FF2_PIECES
                    pe.wait_ge(M["r2_lo"], pairs)
                    pe.wait_ge(M["r2_hi"], pairs)
                for m in range(q * KH // FF2_PIECES, (q + 1) * KH // FF2_PIECES):
                    for part in range(2):
                        mm = pe.matmul(o[:, :], r2[:, part, m, i * P:(i + 1) * P], W["t2"][:, m, :],
                                       start=(m == 0 and part == 0), stop=(m == KH - 1 and part == 1),
                                       skip_group_check=True)
                if q == FF2_PIECES - 1:
                    mm.then_inc(M["F_full0" if i else "C_full"], 1)

            def body(it):
                for s in range(SLOTS):
                    if it.has(0):
                        scores(it.t, it.p, s)
                    ok, t, p, j = lagged(it, s, LAG_T)
                    if ok:
                        transposes(t, p, j)
                    for t, p, m in due(it, FF1_SLOT, s, 1, -1):
                        hidden_low_rank(t, m)
                    ok, t, p, j = lagged(it, s, LAG_PV)
                    if ok and j % GROUP == GROUP - 1:
                        weighted_values(t, p, j // GROUP)
                        if j // GROUP % TILES == TILES - 1:
                            reciprocal_rows(t, j // GROUP // TILES)
                    for t, p, i in due(it, XT_SLOT, s, 0, 1):
                        a_transposes(t, i)
                    for t, p, (i, half) in due(it, V_SLOT, s, 0, 1):
                        values(t, i, half)
                    for t, p, (hg, w) in due(it, QK_SLOT, s, 0, 1):
                        queries_keys(t, hg, w)
                    for t, p, (i, half) in due(it, WO_SLOT, s, 0, -1):
                        out_projection(t, i, half)
                    for t, p, i in due(it, X2_SLOT, s, 0, -1):
                        c_transposes(t, i)
                    for t, p, _ in due(it, Z_SLOT, s, 0, -1):
                        low_rank(t)
                    for t, p, m in due(it, FF1_SLOT, s, 0, -1):
                        hidden(t, m)
                    for t, p, (i, piece) in due(it, FF2_SLOT, s, 0, -1):
                        ff_out(t, i, piece)

            run_iterations(pe, body)

        @block.scalar
        def _(act):
            def exponentials(t, p, j):
                hg, qc, r = block_of(j)
                c0 = key_chunks(p, qc)[0][0] * P
                act.wait_ge(M["S_done"], t * SLOTS + j + 1)
                blk = Sm[:, j % NSM, c0:WIN]
                act.activation(blk, blk, ACT.Exp, bias=nmax[:, j % 8:j % 8 + 1], scale=-1.0,
                               accum_out=sums[:, hg % 2, qc, r:r + 1]).then_inc(M["S_exp"], 1)

            def copy_transposed(t, p, j):
                c0 = key_chunks(p, block_of(j)[1])[0][0] * P
                act.wait_ge(M["T_full"], t * SLOTS + j + 1)
                need(act, M["PT_used"], t * (SLOTS // GROUP) + (j - NPT) // GROUP + 1)
                act.activation(PTs[:, j % NPT, c0:WIN], PTb[:, c0:WIN], ACT.Copy).then_inc(M["PT_copied_act"], 1)

            def sum_rows(t, hg):
                act.wait_ge(M["O_full"], t * NGROUP + hg + 1)
                need(act, M["o32_done"], t * NGROUP + hg)
                act.activation(Rs[:], Ob[:, STEP:2 * STEP], ACT.Copy).then_inc(M["Rs_done"], 1)

            def out_hi(t, hg):
                act.wait_ge(M["o32_done"], t * NGROUP + hg + 1)
                need(act, M["C_full"], (t - 1) * NC + 2)
                act.activation(OT[:, 0, hg, :], o32[:], ACT.Copy).then_inc(M["OT_hi"], 1)

            def a_hi(t, i):
                act.wait_ge(M["a_xn"], t * TILES + i + 1)
                need(act, M["A_full"], t * NA + i if i else (t - 1) * NA + TILES)
                act.activation(xh[:], xn[:], ACT.Copy).then_inc(M["a_xh"], 1)

            def qk_bias(t, hg):
                act.wait_ge(M["A_full"], t * NA + 4 + hg + 1)
                need(act, M["qk_hi_done"], t * NGROUP + hg)
                need(act, M["qk_lo_done"], t * NGROUP + hg)
                act.activation(qk32[:, 0, :], Ab[:, 0:STEP], ACT.Identity, bias=W["bqs"][:, 0, hg:hg + 1],
                               scale=W["c"][:, 0:1])
                act.activation(qk32[:, 1, :], Ab[:, STEP:2 * STEP], ACT.Identity,
                               bias=W["bqs"][:, 1, hg:hg + 1], scale=W["c"][:, 1:2]).then_inc(M["A_free"], 1)

            def b_hi(t, i):
                act.wait_ge(M["b_xn"], t * TILES + i + 1)
                need(act, M["C_full"], t * NC + 2 + i if i else (t - 1) * NC + 2 + TILES)
                act.activation(x2h[:], x2n[:], ACT.Copy).then_inc(M["b_xh"], 1)

            def z_first(t):
                act.wait_ge(M["C_full"], t * NC + 5)
                act.activation(z_h[:], Cb[0:LR, 0:STEP], ACT.Copy).then_inc(M["z_hi"], 1)

            def z_second(t):
                act.wait_ge(M["z_r1"], t + 1)
                act.activation(z_m[:], z_r[:], ACT.Copy).then_inc(M["z_mid"], 1)

            def relu_square(t, m):
                b = m % 2
                act.wait_ge(M[f"F_full{b}"], t * NF[b] + m // 2 + 1)
                need(act, M["r2_sq"], t * (KH // 2) + m)
                need(act, M["r2_hi"], t * (KH // 2) + m)
                for half in range(2):
                    ins = act.activation(r32[:, half * STEP:(half + 1) * STEP],
                                         Fb[b][:, half * STEP:(half + 1) * STEP], ACT.Relu,
                                         scale=W["c1"][:, 2 * m + half:2 * m + half + 1])
                ins.then_inc(M[f"F_free{b}"], 1)
                act.wait_ge(M[f"F_free{b}"], t * NF[b] + m // 2 + 1)
                need(act, M["F_full0"], t * NF[0])
                act.activation(r2[:, 0, 2 * m:2 * m + 2, :].rearrange("p m n -> p (m n)"), r32[:],
                               ACT.Square).then_inc(M["r2_hi"], 1)

            def body(it):
                for s in range(SLOTS):
                    if it.has(0):
                        exponentials(it.t, it.p, s)
                    ok, t, p, j = lagged(it, s, LAG_T)
                    if ok and j % 2 == 0:
                        copy_transposed(t, p, j)
                    ok, t, p, j = lagged(it, s, LAG_O)
                    if ok and j % (TILES * GROUP) == TILES * GROUP - 1:
                        sum_rows(t, block_of(j)[0])
                    ok, t, p, j = lagged(it, s, LAG_OT)
                    if ok and j % (TILES * GROUP) == TILES * GROUP - 1:
                        out_hi(t, block_of(j)[0])
                    for t, p, i in due(it, A_NORM, s, 0, 1):
                        a_hi(t, i)
                    for t, p, (hg, w) in due(it, QK_SLOT, s, 1, 1):
                        if w == 1:
                            qk_bias(t, hg)
                    for t, p, i in due(it, B_NORM, s, 0, -1):
                        b_hi(t, i)
                    for t, p, _ in due(it, Z_SLOT, s, 0, -1):
                        z_first(t)
                    for t, p, _ in due(it, Z_SLOT, s, 1, -1):
                        z_second(t)
                    for t, p, m in due(it, FF1_SLOT, s, 1, -1):
                        relu_square(t, m)

            run_iterations(act, body)

        @block.vector
        def _(v):
            def masked_scores(t, p, j):
                hg, qc, r = block_of(j)
                c0 = key_chunks(p, qc)[0][0] * P
                need(v, M["T_full"], t * SLOTS + j - NSM + 1)
                settled_wait(v, W["consts"], M["S_full"], t * SLOTS + j + 1)
                v.tensor_tensor_reduce(Sm[:, j % NSM, c0:WIN], Sb[j % 2][:, c0:WIN], W["mask"][:, c0:WIN],
                                       W["c"][:, 3:4], 3e38, ALU.add, ALU.min,
                                       nmax[:, j % 8:j % 8 + 1]).then_inc(M["S_done"], 1)

            def copy_transposed(t, p, j):
                c0 = key_chunks(p, block_of(j)[1])[0][0] * P
                v.wait_ge(M["T_full"], t * SLOTS + j + 1)
                need(v, M["PT_used"], t * (SLOTS // GROUP) + (j - NPT) // GROUP + 1)
                v.tensor_copy(PTs[:, j % NPT, c0:WIN], PTb[:, c0:WIN]).then_inc(M["PT_copied_dve"], 1)

            def reciprocals(t, hg):
                v.wait_ge(M["S_exp"], t * SLOTS + (hg + 1) * TILES * GROUP)
                need(v, M["rb_done"], t * NGROUP + hg)
                v.reciprocal(rinv[:].rearrange("p a o -> p (a o)"),
                             sums[:, hg % 2].rearrange("p a r -> p (a r)")).then_inc(M["rinv_done"], 1)
                v.wait_ge(M["rinv_done"], t * NGROUP + hg + 1)
                need(v, M["O_full"], t * NGROUP + hg)
                v.tensor_copy(rb[:], rinv[:].to_broadcast([P, TILES * GROUP, HD])).then_inc(M["rb_done"], 1)

            def normalised(t, hg):
                v.wait_ge(M["Rs_done"], t * NGROUP + hg + 1)
                need(v, M["OT_hi"], t * NGROUP + hg)
                need(v, M["OT_lo"], t * NGROUP + hg)
                v.tensor_tensor(o32[:], Ob[:, 0:STEP], Rs[:], ALU.mult).then_inc(M["o32_done"], 1)

            def ln_stats(k, row, x, n):
                v.bn_stats(lnst[:, row, :], x).then_inc(M[k + "_st"], 1)
                settled_wait(v, W["consts"], M[k + "_st"], n + 1)
                v.bn_aggr(lnmv[:, row, :], lnst[:, row, :]).then_inc(M[k + "_mv"], 1)
                v.wait_ge(M[k + "_mv"], n + 1)

            def a_stats(t, i):
                n = t * TILES + i
                v.wait_ge(M[f"xa_in{i}"], (t + 1) * 16)
                ln_stats("a", 0, xa[:, i, :], n)
                v.tensor_scalar(lnve[:, 0, :], lnmv[:, 0, 1:2], EPS, XS ** -2, ALU.add,
                                ALU.mult).then_inc(M["a_ve"], 1)

            def a_norm(t, i):
                n = t * TILES + i
                v.wait_ge(M["a_rs"], n + 1)
                need(v, M["a_xh"], n)
                need(v, M["a_xl"], n)
                v.tensor_scalar(xn[:], xa[:, i, :], lnmv[:, 0, 0:1], lnrs[:, 0, 0:1], ALU.subtract,
                                ALU.mult).then_inc(M["a_xn"], 1)

            def a_evacuate(t, i):
                v.wait_ge(M["A_full"], t * NA + i + 1)
                v.tensor_copy(xT[:].rearrange("p a k n -> p (a k) n")[:, :, i * P:(i + 1) * P],
                              Ab[:, :].bitcast(F16).rearrange("p (g n) -> p g n", g=2 * KD)
                              ).then_inc(M["A_free"], 1)

            def v_evacuate(t, p, i):
                v.wait_ge(M["A_full"], t * NA + 2 + i + 1)
                need(v, M["PT_used"], (t - 2) * (SLOTS // GROUP))
                v.scalar_tensor_tensor(V[:, p * TILES + i, :], Ab[:, :], W["c"][:, 2:3], W["bv"][:],
                                       ALU.mult, ALU.add).then_inc(M["A_free"], 1)

            def qk_hi(t, hg):
                v.wait_ge(M["A_free"], t * NA + 4 + hg + 1)
                b, c = (hg - 2, t + 1) if hg >= 2 else (hg - 2 + NGROUP, t)
                need(v, M[f"stacked{b}"], c * 3 * GROUP * 16)
                v.tensor_copy(qkp[:, hg % 2, :, 0], qk32[:]).then_inc(M["qk_hi_done"], 1)

            def y_evacuate(t, i):
                n = t * TILES + i
                v.wait_ge(M["C_full"], t * NC + i + 1)
                need(v, M["x1_done"], n)
                v.scalar_tensor_tensor(yb[:], Cb[:, :], W["c"][:, 4:5], W["bo"][:], ALU.mult,
                                       ALU.add).then_inc(M["C_free"], 1)
                v.wait_ge(M["C_free"], t * (NC - 1) + i + 1)
                ln_stats("y", 1, yb[:], n)
                v.tensor_scalar(lnve[:, 1, :], lnmv[:, 1, 1:2], EPS, None, ALU.add).then_inc(M["y_ve"], 1)

            def y_norm(t, i):
                n = t * TILES + i
                v.wait_ge(M["y_rs"], n + 1)
                v.tensor_scalar(yb[:], yb[:], lnmv[:, 1, 0:1], lnrs[:, 1, 0:1], ALU.subtract,
                                ALU.mult).then_inc(M["y_n"], 1)

            def b_stats(t, i):
                n = t * TILES + i
                v.wait_ge(M["x1_done"], n + 1)
                ln_stats("b", 2, x1[:, i, :], n)
                v.tensor_scalar(lnve[:, 2, :], lnmv[:, 2, 1:2], EPS, XS ** -2, ALU.add,
                                ALU.mult).then_inc(M["b_ve"], 1)

            def b_norm(t, i):
                n = t * TILES + i
                v.wait_ge(M["b_rs"], n + 1)
                need(v, M["b_xh"], n)
                need(v, M["b_xl"], n)
                v.tensor_scalar(x2n[:], x1[:, i, :], lnmv[:, 2, 0:1], lnrs[:, 2, 0:1], ALU.subtract,
                                ALU.mult).then_inc(M["b_xn"], 1)

            def b_evacuate(t, i):
                v.wait_ge(M["C_full"], t * NC + 2 + i + 1)
                need(v, M["F_full1"], t * NF[1])
                v.tensor_copy(x2T[:].rearrange("p a k n -> p (a k) n")[:, :, i * P:(i + 1) * P],
                              Cb[:, :].bitcast(F16).rearrange("p (g n) -> p g n", g=2 * KD)
                              ).then_inc(M["C_free"], 1)

            def z_rest(t):
                v.wait_ge(M["z_hi"], t + 1)
                need(v, M["z_done"], t)
                v.scalar_tensor_tensor(z_r[:], z_h[:], W["zsel"][0:LR, 0:1], Cb[0:LR, 0:STEP], ALU.mult,
                                       ALU.add).then_inc(M["z_r1"], 1)

            def z_last(t):
                v.wait_ge(M["z_mid"], t + 1)
                need(v, M["F_full1"], t * NF[1])
                v.scalar_tensor_tensor(z6[:], z_m[:], W["zsel"][0:LR, 1:2], z_r[:], ALU.mult,
                                       ALU.add).then_inc(M["z_done"], 1)

            def square_lo(t, m):
                v.wait_ge(M["r2_sq"], t * (KH // 2) + m + 1)
                v.wait_ge(M["r2_hi"], t * (KH // 2) + m + 1)
                v.tensor_tensor(r2[:, 1, 2 * m:2 * m + 2, :].rearrange("p m n -> p (m n)"), sq32[:],
                                r2[:, 0, 2 * m:2 * m + 2, :].rearrange("p m n -> p (m n)"),
                                ALU.subtract).then_inc(M["r2_lo"], 1)

            def c_evacuate(t, i):
                n = t * TILES + i
                full, free, b = ("F_full0", "F_free0", Fb[0]) if i else ("C_full", "C_free", Cb)
                v.wait_ge(M[full], (t + 1) * (NF[0] if i else NC))
                if i == 0:
                    for k in range(TILES):
                        need(v, M[f"stored{k}"], t * 16)
                v.tensor_tensor(yc[:, i, :], b[:, :], W["s2"][:], ALU.mult).then_inc(M[free], 1)
                v.wait_ge(M[free], (t + 1) * (NF[0] if i else NC - 1))
                ln_stats("c", 3, yc[:, i, :], n)
                v.tensor_scalar(lnve[:, 3, :], lnmv[:, 3, 1:2], EPS, None, ALU.add).then_inc(M["c_ve"], 1)

            def c_norm(t, i):
                n = t * TILES + i
                v.wait_ge(M["c_rs"], n + 1)
                v.tensor_scalar(yc[:, i, :], yc[:, i, :], lnmv[:, 3, 0:1], lnrs[:, 3, 0:1], ALU.subtract,
                                ALU.mult).then_inc(M["c_n"], 1)

            def body(it):
                for s in range(SLOTS):
                    if it.has(0):
                        masked_scores(it.t, it.p, s)
                    ok, t, p, j = lagged(it, s, LAG_T)
                    if ok and j % 2:
                        copy_transposed(t, p, j)
                    ok, t, p, j = lagged(it, s, LAG_RB)
                    if ok and j % (TILES * GROUP) == TILES * GROUP - 1:
                        reciprocals(t, block_of(j)[0])
                    ok, t, p, j = lagged(it, s, LAG_O)
                    if ok and j % (TILES * GROUP) == TILES * GROUP - 1:
                        normalised(t, block_of(j)[0])
                    for t, p, i in due(it, A_STATS, s, 0, 1):
                        a_stats(t, i)
                    for t, p, i in due(it, A_NORM, s, 0, 1):
                        a_norm(t, i)
                    for t, p, i in due(it, XT_SLOT, s, 1, 1):
                        a_evacuate(t, i)
                    for t, p, (i, half) in due(it, V_SLOT, s, 1, 1):
                        if half == 1:
                            v_evacuate(t, p, i)
                    for t, p, (hg, w) in due(it, QK_SLOT, s, 2, 1):
                        if w == 1:
                            qk_hi(t, hg)
                    for t, p, (i, half) in due(it, WO_SLOT, s, 1, -1):
                        if half == 1:
                            y_evacuate(t, i)
                    for t, p, i in due(it, Y_NORM, s, 0, -1):
                        y_norm(t, i)
                    for t, p, i in due(it, B_STATS, s, 0, -1):
                        b_stats(t, i)
                    for t, p, i in due(it, B_NORM, s, 0, -1):
                        b_norm(t, i)
                    for t, p, i in due(it, X2_SLOT, s, 1, -1):
                        b_evacuate(t, i)
                    for t, p, _ in due(it, Z_SLOT, s, 1, -1):
                        z_rest(t)
                    for t, p, _ in due(it, Z_SLOT, s, 2, -1):
                        z_last(t)
                    for t, p, m in due(it, FF1_SLOT, s, 2, -1):
                        square_lo(t, m)
                    for t, p, (i, piece) in due(it, FF2_SLOT, s, 1, -1):
                        if piece == FF2_PIECES - 1:
                            c_evacuate(t, i)
                    for t, p, (i, piece) in due(it, FF2_SLOT, s, 2, -1):
                        if piece == FF2_PIECES - 1:
                            c_norm(t, i)

            run_iterations(v, body)

        @block.gpsimd
        def _(g):
            def rstd(k, row, n):
                g.wait_ge(M[k + "_ve"], n + 1)
                g.tensor_tensor(lnrs[:, row, 0:1], lnve[:, row, :], W["nhalf"][:], ALU.pow).then_inc(M[k + "_rs"], 1)

            def a_lo(t, i):
                n = t * TILES + i
                g.wait_ge(M["a_xh"], n + 1)
                need(g, M["A_full"], t * NA + i if i else (t - 1) * NA + TILES)
                g.tensor_tensor(xl[:], xn[:], xh[:], ALU.subtract).then_inc(M["a_xl"], 1)

            def qk_lo(t, hg):
                g.wait_ge(M["qk_hi_done"], t * NGROUP + hg + 1)
                need(g, M["S_full"], (t - 1) * SLOTS + (hg + 1) * TILES * GROUP)
                g.tensor_tensor(qkp[:, hg % 2, :, 1], qk32[:], qkp[:, hg % 2, :, 0],
                                ALU.subtract).then_inc(M["qk_lo_done"], 1)

            def out_lo(t, hg):
                g.wait_ge(M["OT_hi"], t * NGROUP + hg + 1)
                g.tensor_tensor(OT[:, 1, hg, :], o32[:], OT[:, 0, hg, :], ALU.subtract).then_inc(M["OT_lo"], 1)

            def first_residual(t, i):
                n = t * TILES + i
                g.wait_ge(M["y_n"], n + 1)
                g.wait_ge(M[f"xr_in{i}"], (t + 1) * 16)
                need(g, M["c_out"], (t - 1) * TILES + i + 1)
                g.tensor_tensor(x1[:, i, :], yb[:], xr[:, i, :], ALU.add).then_inc(M["x1_done"], 1)

            def b_lo(t, i):
                n = t * TILES + i
                g.wait_ge(M["b_xh"], n + 1)
                need(g, M["C_full"], t * NC + 2 + i if i else (t - 1) * NC + 2 + TILES)
                g.tensor_tensor(x2l[:], x2n[:], x2h[:], ALU.subtract).then_inc(M["b_xl"], 1)

            def square(t, m):
                g.wait_ge(M[f"F_free{m % 2}"], t * NF[m % 2] + m // 2 + 1)
                need(g, M["r2_lo"], t * (KH // 2) + m)
                g.tensor_tensor(sq32[:], r32[:], r32[:], ALU.mult).then_inc(M["r2_sq"], 1)

            def second_residual(t, i):
                n = t * TILES + i
                g.wait_ge(M["c_n"], n + 1)
                g.tensor_tensor(yc[:, i, :], yc[:, i, :], x1[:, i, :], ALU.add).then_inc(M["c_out"], 1)

            def body(it):
                for s in range(SLOTS):
                    ok, t, p, j = lagged(it, s, LAG_OT)
                    if ok and j % (TILES * GROUP) == TILES * GROUP - 1:
                        out_lo(t, block_of(j)[0])
                    for t, p, i in due(it, A_STATS, s, 0, 1):
                        rstd("a", 0, t * TILES + i)
                    for t, p, i in due(it, A_NORM, s, 0, 1):
                        a_lo(t, i)
                    for t, p, (hg, w) in due(it, QK_SLOT, s, 2, 1):
                        if w == 1:
                            qk_lo(t, hg)
                    for t, p, (i, half) in due(it, WO_SLOT, s, 1, -1):
                        if half == 1:
                            rstd("y", 1, t * TILES + i)
                    for t, p, i in due(it, Y_NORM, s, 0, -1):
                        first_residual(t, i)
                    for t, p, i in due(it, B_STATS, s, 0, -1):
                        rstd("b", 2, t * TILES + i)
                    for t, p, i in due(it, B_NORM, s, 0, -1):
                        b_lo(t, i)
                    for t, p, m in due(it, FF1_SLOT, s, 1, -1):
                        square(t, m)
                    for t, p, (i, piece) in due(it, FF2_SLOT, s, 1, -1):
                        if piece == FF2_PIECES - 1:
                            rstd("c", 3, t * TILES + i)
                    for t, p, (i, piece) in due(it, FF2_SLOT, s, 2, -1):
                        if piece == FF2_PIECES - 1:
                            second_residual(t, i)

            run_iterations(g, body)


def build(nc, A, out):
    with ExitStack() as ctx:
        def sb(name, shape, dt):
            return ctx.enter_context(nc.sbuf_tensor(name, shape, dt))

        W = {
            "w": sb("w_attn", [P, 4, 2, KD, D], F16),
            "t1": sb("t1", [P, KD, HIDDEN], F16),
            "t2": sb("t2", [P, KH, D], F16),
            "u": sb("u_T", [LR, HIDDEN], BF16),
            "v": sb("v_T", [P, 2, KD, LR], F16),
            "bo": sb("bo_rows", [P, D], F32), "bv": sb("bv_rows", [P, D], F32),
            "s2": sb("s2_rows", [P, D], F32),
            "mask": sb("mask", [P, WIN], F32),
            "idf": sb("idf", [P, P], F32), "idh": sb("idh", [P, P], F16), "idb": sb("idb", [P, P], BF16),
            "nhalf": sb("nhalf", [P, 1], F32), "zsel": sb("zsel", [P, 2], F32),
            "c": sb("scales", [P, 12], F32), "c1": sb("c1", [P, KH], F32),
            "bqs": sb("bqs", [P, 2, KD], F32),
            "consts": ctx.enter_context(nc.semaphore("consts_ready")),
        }
        prepare(nc, A, W)
        steps(nc, A, W, out)



def kernel(**inputs):
    import numpy as np
    import concourse.bacc as bacc
    from concourse.bass_utils import run_bass_kernel_spmd

    nc = bacc.Bacc("TRN2", target_bir_lowering=False, num_devices=1)
    arrays, A = {}, {}
    for name, a in inputs.items():
        short = name.replace("L0_attn_", "").replace("L0_ffn_", "")
        a = np.ascontiguousarray(a)
        if short == "x":
            a = a.reshape(BATCH * SEQ, D)
        if short == "gate":
            a = a.reshape(1)
        arrays[f"in_{short}"] = a
        A[short] = nc.dram_tensor(f"in_{short}", a.shape, mybir.dt.from_np(a.dtype), kind="ExternalInput").ap()
    out = nc.dram_tensor("out_0", (BATCH * SEQ, D), F32, kind="ExternalOutput").ap()
    build(nc, A, out)
    r = run_bass_kernel_spmd(nc, [arrays], core_ids=[0])
    return r.results[0]["out_0"].reshape(BATCH, SEQ, D)
```

```python
from contextlib import ExitStack

import concourse.bass as bass
from concourse import mybir

P = 128
BATCH, SEQ, D = 8, 1024, 512
HEADS, HD = 16, 32
HIDDEN, RANK = 2048, 16
WINDOW = 256
STEP = 256
TILES = STEP // P
PER_SEQ = SEQ // STEP
NSTEP = BATCH * PER_SEQ
KD = D // P
KH = HIDDEN // P
GROUP = P // HD
NGROUP = HEADS // GROUP
SLOTS = NGROUP * TILES * GROUP
NKC = WINDOW // P + 1
WIN = NKC * P
RING = 2 * STEP
ST = 3 * HD
LR = 6 * RANK
EPS = 1e-5
XS = 2.0 ** 11
NEG = -1e38

F32, F16, BF16, U32 = mybir.dt.float32, mybir.dt.float16, mybir.dt.bfloat16, mybir.dt.uint32
ALU, ACT, AX = mybir.AluOpType, mybir.ActivationFunctionType, mybir.AxisListType
RADD, RMAX = bass.bass_isa.ReduceOp.add, bass.bass_isa.ReduceOp.max

XT_SLOT = {3: 0, 6: 1}
V_SLOT = {7: (0, 0), 8: (0, 1), 12: (1, 0), 13: (1, 1)}
QK_SLOT = {14: (0, 0), 15: (0, 1), 17: (1, 0), 20: (1, 1), 25: (2, 0), 29: (2, 1), 32: (3, 0), 33: (3, 1)}
X_SLOT = {22: 0}
XR_SLOT = {1: 0, 8: 1}
WO_SLOT = {5: (0, 0), 6: (0, 1), 9: (1, 0), 10: (1, 1)}
X2_SLOT = {13: 0, 14: 1}
Z_SLOT = {16: 0}
FF1_SLOT = {18: 0, 19: 1, 21: 2, 22: 3, 23: 4, 24: 5, 25: 6, 26: 7}
FF2_PIECES = 4
FF2_SLOT = {25: (0, 0), 27: (0, 1), 28: (0, 2), 30: (0, 3), 31: (1, 0), 32: (1, 1), 34: (1, 2), 36: (1, 3)}
A_STATS, A_NORM = {1: 0, 4: 1}, {2: 0, 5: 1}
Y_NORM, B_STATS, B_NORM = {8: 0, 12: 1}, {9: 0, 13: 1}, {10: 0, 14: 1}
LAG_T, LAG_PV = 2, 3
LAG_RB, LAG_O, LAG_OT = 1, 3, 4


def need(eng, sem, value):
    if isinstance(value, int) and value <= 0:
        return
    eng.wait_ge(sem, value)


def settled_wait(eng, consts, sem, value):
    if not isinstance(value, int):
        value = eng.to_reg(value)
    eng.wait_ge(consts, 1)
    eng.wait_ge(sem, value)


class Iteration:

    def __init__(self, t, p):
        self.t, self.p = t, p

    def has(self, k):
        return not isinstance(self.t, int) or 0 <= self.t + k < NSTEP

    def step(self, k):
        return self.t + k, (self.p + k) % PER_SEQ


def run_iterations(eng, body):
    for t in range(-1, 2):
        body(Iteration(t, t % PER_SEQ))
    n = NSTEP // PER_SEQ - 1
    with eng.Fori(0, n, 1) as i:
        for q in range(PER_SEQ):
            body(Iteration(i * PER_SEQ + (2 + q), (2 + q) % PER_SEQ))
    for t in range(2 + n * PER_SEQ, NSTEP + 2):
        body(Iteration(t, t % PER_SEQ))


def due(it, table, slot, lag, base):
    for back in range(3):
        entry = table.get(slot - lag + back * SLOTS)
        if entry is not None and it.has(base - back):
            yield (*it.step(base - back), entry)


def lagged(it, slot, lag):
    j = slot - lag
    back = 0 if j >= 0 else 1
    return (it.has(-back), *it.step(-back), j + back * SLOTS)


def block_of(j):
    return j // (TILES * GROUP), j // GROUP % TILES, j % GROUP


def key_chunks(p, qc):
    c = p * TILES + qc
    return [(i, c - NKC + 1 + i) for i in range(NKC) if c - NKC + 1 + i >= 0]


def prepare(nc, A, W):
    with ExitStack() as ctx:
        def sb(name, shape, dt):
            return ctx.enter_context(nc.sbuf_tensor(name, shape, dt))

        def sem(name):
            return ctx.enter_context(nc.semaphore(name))

        NSTAGE = 6
        stage = [sb(f"stage{i}", [P, 4 * D], F32) for i in range(NSTAGE)]
        NS = 4
        s_hi = [sb(f"s_hi{i}", [P, 4 * D], F16) for i in range(NS)]
        s_lo = [sb(f"s_lo{i}", [P, 4 * D], F16) for i in range(NS)]
        junk = [sb(f"junk{i}", [P, 4 * D], F16) for i in range(2)]
        idb = sb("idb", [P, P], BF16)
        u_in = sb("u_in", [P, KH, RANK], F32)
        u_sc = sb("u_sc", [P, KH, RANK], F32)
        u_r = sb("u_r", [P, KH, RANK], F32)
        u_part = sb("u_part", [P, 3, KH, RANK], BF16)
        u_stack = sb("u_stack", [P, KH, LR], BF16)
        v_in = sb("v_in", [RANK, D], F32)
        fbT = sb("fbT", [RANK, RANK], F32)
        fb6 = sb("fb6", [RANK, LR], F32)
        vp = sb("vp", [P, KD, LR], F32)
        vsq = sb("vsq", [P, KD, RANK], F32)
        usq = sb("usq", [P, KH], F32)
        gate = sb("gate", [P, 1], F32)
        bqk = sb("bqk", [P, 2, KD], F32)
        red = sb("red", [P, 16], F32)
        redA = sb("redA", [P, 16], F32)
        vss = sb("vss", [P, 2], F32)
        bnd = sb("bnd", [P, 9], F32)
        p2 = sb("p2", [P, 9], F32)
        inv = sb("inv", [P, 9], F32)
        pow_in = sb("pow_in", [P, 2], F32)
        pow_ex = sb("pow_ex", [P, 2], F32)
        pow_out = sb("pow_out", [P, 2], F32)
        g23 = sb("g23", [P, 2], F32)
        s1 = sb("s1", [P, KH], F32)
        s2 = sb("s2", [P, KD], F32)
        h1 = sb("h1", [P, 2, KH], F32)
        h2 = sb("h2", [P, 2, KD], F32)
        fac = sb("fac", [P, KH], F32)
        s2c = sb("s2c", [P, KD], F32)
        sW = sb("sW", [P, 4], F32)
        ps = [ctx.enter_context(nc.psum_tensor(f"pp{i}", [P, 512], F32)) for i in range(4)]

        loaded = [sem(f"loaded{i}") for i in range(NSTAGE)]
        s_small = sem("small_loaded")
        s_pool = sem("pool_ready")
        dch = sem("dve_step")
        s_hi_done = sem("hi_done")
        s_act_hi = sem("weights_hi")
        s_scales = sem("weight_scales_ready")
        s_sums = sem("abs_sums")
        s_bounds = sem("bound_inputs")
        s_pt = sem("prep_transposed")
        s_ev = {"dve": sem("prep_evacuated_dve"), "act": sem("prep_evacuated_act")}
        s_red = sem("red_ready")
        s_red_all = sem("red_all")
        block = ctx.enter_context(nc.Block())

        src = ([w.rearrange("(c p) i -> p c i", p=P) for w in (A["Wq"], A["Wk"], A["Wv"], A["Wo"])]
               + [A["w_fc"].rearrange("(m p) i -> p m i", p=P)[:, 4 * n:4 * n + 4, :] for n in range(4)]
               + [A["w_proj"].rearrange("(c p) h -> p c h", p=P)[:, n:n + 1, :] for n in range(4)])
        NW = 4

        def piece(n):
            return stage[n % NSTAGE][:, :]

        def wait_loaded(eng, n):
            eng.wait_ge(loaded[n % NSTAGE], 16 * (n // NSTAGE + 1))

        @block.sync
        def _(sp):
            for n, a in enumerate(src):
                if n == 2:
                    sp.dma_start(u_in[:], A["u"].rearrange("(m p) r -> p m r", p=P)).then_inc(s_small, 16)
                    sp.dma_start(v_in[:], A["v"]).then_inc(s_small, 16)
                    with nc.allow_non_contiguous_dma(reason="256 words"):
                        sp.dma_start(fbT[:], A["fast_b"].rearrange("a r -> r a")).then_inc(s_small, 16)
                        sp.dma_start(bqk[:, 0, :], A["bq"].rearrange("(c p) -> p c", p=P)).then_inc(s_small, 16)
                        sp.dma_start(bqk[:, 1, :], A["bk"].rearrange("(c p) -> p c", p=P)).then_inc(s_small, 16)
                    sp.dma_start(gate[:], A["gate"].rearrange("(a b) -> a b", a=1).to_broadcast([P, 1])).then_inc(s_small, 16)
                    sp.dma_start(W["bv"][:], A["bv"].rearrange("(a d) -> a d", a=1).to_broadcast([P, D])).then_inc(s_small, 16)
                    sp.dma_start(W["bo"][:], A["bo"].rearrange("(a d) -> a d", a=1).to_broadcast([P, D])).then_inc(s_small, 16)
                if n >= NSTAGE:
                    sp.wait_ge(s_hi_done, n - NSTAGE + 1)
                d = piece(n).rearrange("p (c i) -> p c i", c=a.shape[1])
                sp.dma_start(d, a).then_inc(loaded[n % NSTAGE], 16)

        @block.gpsimd
        def _(g):
            g.memset(W["idf"][:], 0.0)
            g.memset(W["mask"][:], 0.0)
            g.memset(W["nhalf"][:], -0.5).then_inc(W["consts"], 1)
            g.memset(W["zsel"][:], -1.0)
            g.memset(pow_ex[:], 0.5).then_inc(s_pool, 1)
            g.wait_ge(s_pool, 1)
            g.affine_select(out=W["idf"][:], in_=W["idf"][:], compare_op=ALU.not_equal, fill=1.0, base=0,
                            pattern=[[-1, P]], channel_multiplier=1)
            m0, m2 = W["mask"][:, 0:P], W["mask"][:, WIN - P:WIN]
            g.affine_select(out=m0, in_=m0, compare_op=ALU.is_gt, fill=NEG, base=0,
                            pattern=[[1, P]], channel_multiplier=-1)
            g.affine_select(out=m2, in_=m2, compare_op=ALU.is_ge, fill=NEG, base=0,
                            pattern=[[-1, P]], channel_multiplier=1)
            for col, group in ((0, 3), (1, 5)):
                zs = W["zsel"][:, col:col + 1]
                last = g.affine_select(out=zs, in_=zs, compare_op=ALU.is_ge, fill=0.0, base=-group * RANK,
                                       pattern=[[0, 1]], channel_multiplier=1)
            last.then_inc(s_pool, 1)
            g.wait_ge(s_pool, 2)
            g.tensor_copy(W["idh"][:], W["idf"][:])
            g.tensor_copy(idb[:], W["idf"][:]).then_inc(s_pool, 1)
            for n, (c0, c1) in enumerate(((0, 2), (2, 4), (4, 9))):
                g.wait_ge(s_red, n + 1)
                g.partition_all_reduce(redA[:, c0:c1], red[:, c0:c1], P, RMAX).then_inc(s_red_all, 1)
            g.wait_ge(s_red, 4)
            g.partition_all_reduce(vss[:, 1:2], vss[:, 0:1], P, RADD).then_inc(s_red_all, 1)
            g.wait_ge(s_bounds, 1)
            g.tensor_tensor(pow_out[:], pow_in[:], pow_ex[:], ALU.pow).then_inc(s_red_all, 1)

        jobs = ([("w", n, c) for n in range(NW) for c in range(4)] + ["vp"]
                + [("t1", n, h) for n in range(4) for h in range(2)]
                + [("t2", n, h) for n in range(4) for h in range(2)] + ["s2"] + [("u", h) for h in range(2)])
        T_JOB = jobs.index(("t1", 0, 0))
        S2_JOB = jobs.index("s2")

        def owner(n):
            return "act" if jobs[n][0] in ("t1", "t2") or (jobs[n][0] == "w" and n % 2) else "dve"

        def rank(n):
            return sum(owner(k) == owner(n) for k in range(n + 1))

        def evacuate(eng, who, n0, n1):
            for n in range(n0, n1):
                if owner(n) != who:
                    continue
                job, b = jobs[n], ps[n % 4]
                bh = b[:, :].bitcast(F16)
                if job == "vp":
                    dst, a = vp[:].rearrange("p k c -> p (k c)"), b[:, 0:KD * LR]
                elif job == "s2":
                    dst, a = W["s2"][:], b[:, :]
                elif job[0] == "t1":
                    m = 4 * job[1] + 2 * job[2]
                    dst, a = W["t1"][:, :, m * P:(m + 2) * P], bh.rearrange("p (k c) -> p k c", k=KD)
                elif job[0] == "t2":
                    _, c, h = job
                    dst = W["t2"][:, 8 * h:8 * h + 8, c * P:(c + 1) * P]
                    a = bh.rearrange("p (m c) -> p m c", m=8)
                elif job[0] == "u":
                    h = job[1]
                    dst, a = W["u"][:, 8 * h * P:(8 * h + 8) * P], b[0:LR, :].bitcast(BF16)
                else:
                    _, w, c = job
                    dst = W["w"][:, w].rearrange("p a k o -> p (a k) o")[:, :, c * P:(c + 1) * P]
                    a = bh.rearrange("p (g c) -> p g c", g=2 * KD)
                eng.wait_ge(s_pt, n + 1)
                ins = eng.tensor_copy(dst, a) if who == "dve" else eng.activation(dst, a, ACT.Copy)
                ins.then_inc(s_ev[who], 1)

        @block.tensor
        def _(pe):
            pe.wait_ge(s_pool, 3)
            for n, job in enumerate(jobs):
                if n >= 4:
                    pe.wait_ge(s_ev[owner(n - 4)], rank(n - 4))
                b = ps[n % 4]
                bh = b[:, :].bitcast(F16)
                if job == "vp":
                    pe.wait_ge(dch, 1)
                    for k in range(KD):
                        last = pe.matmul(b[:, k * LR:(k + 1) * LR], v_in[:, k * P:(k + 1) * P], fb6[:],
                                         start=True, stop=True)
                elif job == "s2":
                    pe.wait_ge(s_red, 5)
                    for c in range(KD):
                        last = pe.transpose(b[:, c * P:(c + 1) * P], s2c[:, c:c + 1].to_broadcast([P, P]),
                                            W["idf"][:])
                elif job[0] == "t1":
                    _, n4, h = job
                    pe.wait_ge(s_hi_done, NW + n4 + 1)
                    for k in range(KD):
                        for mm in range(2):
                            m = 2 * h + mm
                            last = pe.transpose(bh[:, k * 256 + mm * P:k * 256 + mm * P + P],
                                                s_hi[n4 % NS][:, m * D + k * P:m * D + k * P + P], W["idh"][:])
                elif job[0] == "t2":
                    _, c, h = job
                    pe.wait_ge(s_hi_done, NW + 4 + c + 1)
                    for m in range(8):
                        last = pe.transpose(bh[:, m * P:m * P + P],
                                            s_hi[c % NS][:, (8 * h + m) * P:(8 * h + m + 1) * P], W["idh"][:])
                elif job[0] == "u":
                    h = job[1]
                    pe.wait_ge(s_red, 6)
                    bb = b[:, :].bitcast(BF16)
                    for m in range(8):
                        last = pe.transpose(bb[0:LR, m * P:m * P + P], u_stack[:, 8 * h + m, :], idb[:])
                else:
                    _, w, c = job
                    pe.wait_ge(s_hi_done, w + 1)
                    for part, t in enumerate((s_hi, s_lo)):
                        for k in range(KD):
                            last = pe.transpose(bh[:, (part * KD + k) * P:(part * KD + k + 1) * P],
                                                t[w % NS][:, c * D + k * P:c * D + k * P + P], W["idh"][:])
                last.then_inc(s_pt, 1)

        @block.scalar
        def _(act):
            for w in range(NW):
                act.wait_ge(s_scales, w // 2 + 1)
                act.activation(s_hi[w][:], piece(w), ACT.Identity, scale=sW[:, w:w + 1]).then_inc(s_act_hi, 1)
            for m in range(8):
                n = NW + m
                s, w = (s1, 4) if m < 4 else (s2, 1)
                c0 = w * (m % 4)
                if m < 2:
                    evacuate(act, "act", 4 * m, 4 * m + 4)
                if m == 2:
                    evacuate(act, "act", 8, 16)
                wait_loaded(act, n)
                if m >= 2:
                    act.wait_ge(s_sums, m - 1)
                for c in range(w):
                    cols = slice(c * 4 * D // w, (c + 1) * 4 * D // w)
                    ins = act.activation(junk[m % 2][:, cols], piece(n)[:, cols], ACT.Abs,
                                         accum_out=s[:, c0 + c:c0 + c + 1])
                ins.then_inc(s_sums, 1)
                if m >= 2:
                    evacuate(act, "act", T_JOB + 2 * (m - 2), T_JOB + 2 * (m - 1))
            evacuate(act, "act", T_JOB + 12, T_JOB + 16)

        @block.vector
        def _(v):
            count = {}

            def then(ins, sem=dch):
                count[sem.name] = count.get(sem.name, 0) + 1
                ins.then_inc(sem, 1)
                v.wait_ge(sem, count[sem.name])

            def inverse_powers(c0, c1):
                then(v.tensor_scalar(bnd[:, c0:c1], bnd[:, c0:c1], 1e-20, None, ALU.max))
                then(v.tensor_scalar(p2[:, c0:c1].bitcast(U32), bnd[:, c0:c1].bitcast(U32), 0x7F800000, None,
                                     ALU.bitwise_and))
                then(v.reciprocal(inv[:, c0:c1], p2[:, c0:c1]))

            for n in range(NW):
                wait_loaded(v, n)
                last = v.tensor_reduce(red[:, n:n + 1], piece(n), AX.X, ALU.max, apply_absolute_value=True)
                if n % 2:
                    last.then_inc(s_red, 1)
                    count[s_red.name] = n // 2 + 1
                if n == 1:
                    v.wait_ge(s_small, 16 * 8)
                    then(v.tensor_copy(fb6[:].rearrange("p (g r) -> p g r", g=6),
                                       fbT[:].rearrange("p (g r) -> p g r", g=1).to_broadcast([RANK, 6, RANK])))
                    then(v.tensor_tensor(u_sc[:], u_in[:], u_in[:], ALU.mult))
                    then(v.tensor_reduce(usq[:], u_sc[:], AX.X, ALU.add))
                    v.tensor_reduce(red[:, 8:9], usq[:], AX.X, ALU.max)
                    v.tensor_reduce(red[:, 4:6], bqk[:], AX.X, ALU.max, apply_absolute_value=True)
                    v.tensor_reduce(red[:, 6:7], W["bv"][:], AX.X, ALU.max, apply_absolute_value=True)
            for half in range(2):
                c0 = 2 * half
                v.wait_ge(s_red_all, half + 1)
                then(v.tensor_copy(bnd[:, c0:c0 + 2], redA[:, c0:c0 + 2]))
                inverse_powers(c0, c0 + 2)
                v.tensor_scalar(sW[:, c0:c0 + 2], inv[:, c0:c0 + 2], 2.0 ** 14, None, ALU.mult).then_inc(s_scales, 1)
            for w in range(NW):
                v.wait_ge(s_act_hi, w + 1)
                v.scalar_tensor_tensor(s_lo[w][:], piece(w), sW[:, w:w + 1], s_hi[w][:], ALU.mult,
                                       ALU.subtract).then_inc(s_hi_done, 1)
                if w >= 2:
                    evacuate(v, "dve", 4 * (w - 2), 4 * (w - 1))
            count[s_hi_done.name] = NW
            for m in range(8):
                n = NW + m
                s, h, w = (s1, h1, 4) if m < 4 else (s2, h2, 1)
                c0 = w * (m % 4)
                pc = piece(n).rearrange("p (c i) -> p c i", c=w)
                v.wait_ge(s_sums, m + 1)
                then(v.tensor_scalar(s[:, c0:c0 + w], s[:, c0:c0 + w], w / (4.0 * D), EPS, ALU.mult, ALU.max))
                v.tensor_scalar(h[:, 0, c0:c0 + w], s[:, c0:c0 + w], -0.5, None, ALU.mult)
                then(v.tensor_scalar(h[:, 1, c0:c0 + w], s[:, c0:c0 + w], 0.5, None, ALU.mult))
                if m == 2:
                    evacuate(v, "dve", T_JOB - 1, T_JOB)
                v.wait_ge(s_pt, T_JOB + 2 * (m - NS + 1) if m >= NS else 4 * (m + 1))
                o = s_hi[m % NS][:].rearrange("p (c i) -> p c i", c=w)
                below = s_lo[m % NS][:].rearrange("p (c i) -> p c i", c=w)
                for c in range(w):
                    last = v.tensor_scalar(below[:, c], pc[:, c], h[:, 0, c0 + c:c0 + c + 1], None, ALU.is_lt)
                then(last)
                for c in range(w):
                    last = v.scalar_tensor_tensor(o[:, c], pc[:, c], h[:, 1, c0 + c:c0 + c + 1], below[:, c],
                                                  ALU.is_gt, ALU.subtract)
                then(last, s_hi_done)
                if m < 2:
                    evacuate(v, "dve", 8 + 4 * m, 12 + 4 * m)
                if m == 3:
                    then(v.tensor_reduce(red[:, 7:8], s1[:], AX.X, ALU.max), s_red)
            v.wait_ge(s_ev["dve"], rank(T_JOB - 1))
            then(v.tensor_tensor(vsq[:], vp[:, :, 0:RANK], vp[:, :, 0:RANK], ALU.mult))
            then(v.tensor_reduce(vss[:, 0:1], vsq[:], AX.XY, ALU.add), s_red)
            v.wait_ge(s_red_all, 4)
            v.tensor_tensor(pow_in[:, 0:1], redA[:, 8:9], vss[:, 1:2], ALU.mult)
            then(v.tensor_copy(pow_in[:, 1:2], vss[:, 1:2]), s_bounds)
            v.scalar_tensor_tensor(bnd[:, 4:7], redA[:, 0:3], 1.01 * D, redA[:, 4:7], ALU.mult, ALU.add)
            then(v.scalar_tensor_tensor(g23[:, 0:1], gate[:], -1.0, gate[:], ALU.mult, ALU.max))
            v.wait_ge(s_red_all, 5)
            v.tensor_scalar(bnd[:, 7:8], pow_out[:, 1:2], 1.01, None, ALU.mult)
            then(v.scalar_tensor_tensor(g23[:, 1:2], g23[:, 0:1], 23.0, pow_out[:, 0:1], ALU.mult, ALU.mult))
            then(v.scalar_tensor_tensor(bnd[:, 8:9], redA[:, 7:8], 1.01 * D, g23[:, 1:2], ALU.mult, ALU.add))
            inverse_powers(4, 9)
            c = W["c"]
            v.tensor_tensor(c[:, 0:3], inv[:, 4:7], p2[:, 0:3], ALU.mult)
            v.tensor_tensor(c[:, 3:4], p2[:, 4:5], p2[:, 5:6], ALU.mult)
            v.tensor_scalar(c[:, 5:8], inv[:, 4:7], 2.0 ** 14, None, ALU.mult)
            v.tensor_scalar(c[:, 8:9], inv[:, 8:9], 2.0 ** 6 / XS, None, ALU.mult)
            v.tensor_tensor(c[:, 9:10], p2[:, 8:9], p2[:, 8:9], ALU.mult)
            v.tensor_scalar(c[:, 10:11], inv[:, 7:8], 2.0 ** 14, None, ALU.mult)
            v.tensor_scalar(c[:, 11:12], p2[:, 7:8], 2.0 ** -14, gate[:, 0:1], ALU.mult, ALU.mult)
            v.reciprocal(fac[:], s1[:])
            then(v.tensor_tensor(c[:, 4:5], p2[:, 6:7], p2[:, 3:4], ALU.mult))
            v.tensor_scalar(c[:, 0:3], c[:, 0:3], 1.0 / XS, None, ALU.mult)
            v.tensor_scalar(c[:, 3:4], c[:, 3:4], -(float(HD) ** -0.5) * 2.0 ** -28, None, ALU.mult)
            v.tensor_scalar(c[:, 4:5], c[:, 4:5], 2.0 ** -28, None, ALU.mult)
            v.tensor_scalar(W["bqs"][:, 0, :], bqk[:, 0, :], c[:, 5:6], None, ALU.mult)
            v.tensor_scalar(W["bqs"][:, 1, :], bqk[:, 1, :], c[:, 6:7], None, ALU.mult)
            v.tensor_scalar(W["bv"][:], W["bv"][:], c[:, 7:8], None, ALU.mult)
            v.tensor_scalar(W["c1"][:], s1[:], c[:, 8:9], None, ALU.mult)
            v.tensor_scalar(fac[:], fac[:], c[:, 11:12], None, ALU.mult)
            then(v.tensor_scalar(vp[:], vp[:], c[:, 10:11], None, ALU.mult))
            v.tensor_scalar(s2c[:], s2[:], c[:, 9:10], 2.0 ** -12, ALU.mult, ALU.mult).then_inc(s_red, 1)
            then(v.tensor_copy(W["v"][:, 0], vp[:]))
            v.tensor_tensor(W["v"][:, 1], vp[:], W["v"][:, 0], ALU.subtract)
            then(v.tensor_tensor(u_sc[:], u_in[:],
                                 fac[:].rearrange("p (m o) -> p m o", o=1).to_broadcast([P, KH, RANK]), ALU.mult))
            then(v.tensor_copy(u_part[:, 0], u_sc[:]))
            then(v.tensor_tensor(u_r[:], u_sc[:], u_part[:, 0], ALU.subtract))
            then(v.tensor_copy(u_part[:, 1], u_r[:]))
            then(v.tensor_tensor(u_part[:, 2], u_r[:], u_part[:, 1], ALU.subtract))
            for g, part in enumerate((0, 1, 2, 0, 1, 0)):
                last = v.tensor_copy(u_stack[:, :, g * RANK:(g + 1) * RANK], u_part[:, part])
            last.then_inc(s_red, 1)
            evacuate(v, "dve", S2_JOB, S2_JOB + 3)


def steps(nc, A, W, out):
    with ExitStack() as ctx:
        def sb(name, shape, dt):
            return ctx.enter_context(nc.sbuf_tensor(name, shape, dt))

        def bank(name):
            return ctx.enter_context(nc.psum_tensor(name, [P, 512], F32))

        def sem(name):
            return ctx.enter_context(nc.semaphore(name))

        xa = sb("xa", [P, TILES, D], F32)
        xn = sb("xn", [P, TILES, D], F32)
        xT = sb("xT", [P, 2, KD, STEP], F16)
        qk32 = sb("qk32", [P, 2, 2, STEP], F32)
        qkp = sb("qkp", [P, 2, 2, 2, STEP], F16)
        QK3 = sb("QK3", [ST, HEADS, 1 + RING // STEP, STEP], F16)
        Q3, K3 = QK3[:, :, 0, :], QK3[:, :, 1:, :].rearrange("p h b n -> p h (b n)")
        V = sb("V", [P, SEQ // P, D], F32)
        NSM, NPT = 4, 8
        Sm = sb("Sm", [P, NSM, WIN], F32)
        nmax = sb("nmax", [P, 8], F32)
        sums = sb("sums", [P, 2, TILES, GROUP], F32)
        PTs = sb("PTs", [P, NPT, WIN], F32)
        rinv = sb("rinv", [P, TILES * GROUP, 1], F32)
        rb = sb("rb", [P, TILES * GROUP, HD], F32)
        Rs = sb("Rs", [P, STEP], F32)
        o32 = sb("o32", [P, STEP], F32)
        OT = sb("OT", [P, 2, NGROUP, STEP], F16)
        yb = sb("yb", [P, TILES, D], F32)
        x1 = sb("x1", [P, TILES, D], F32)
        x2n = sb("x2n", [P, TILES, D], F32)
        x2T = sb("x2T", [P, 2, KD, STEP], F16)
        z_h, z_m, z6 = (sb(n, [LR, STEP], BF16) for n in ("z_h", "z_m", "z6"))
        z_r = sb("z_r", [LR, STEP], F32)
        r32, sq32 = sb("r32", [P, 2, 2 * STEP], F32), sb("sq32", [P, 2 * STEP], F32)
        r2 = sb("r2", [P, 2, KH, STEP], F16)
        yc = sb("yc", [P, TILES, D], F32)
        lnst = sb("lnst", [P, 4, 6], F32)
        lnmv = sb("lnmv", [P, 4, 2], F32)
        lnve = sb("lnve", [P, 4, 1], F32)
        lnrs = sb("lnrs", [P, 4, 2], F32)

        Sb = [bank("S0"), bank("S1")]
        PTb, Ob = bank("PTb"), bank("Ob")
        Fb = [bank("F0"), bank("F1")]
        Ab, Cb = bank("Ab"), bank("Cb")

        names = """xa_in0 xa_in1 a_st a_mv a_ve a_rs a_xn a_xh
            A_full A_free  qk_hi_done qk_lo_done stacked0 stacked1 stacked2 stacked3
            S_full S_done S_exp T_full PT_copied_act PT_copied_dve PT_used rinv_done rb_done O_full Rs_done o32_done
            OT_hi OT_lo
            xr_in0 xr_in1 y_done y_st y_mv y_ve y_rs y_n x1_done b_st b_mv b_ve b_rs b_xn b_xh
            C_full C_free z_hi z_r1 z_mid z_done F_full0 F_full1 F_free0 F_free1 relu_done r2_hi r2_sq r2_lo
            c_y c_st c_mv c_ve c_rs c_n c_out stored0 stored1""".split()
        M = {n: sem(n) for n in names}

        def copied(eng, t, j):
            need(eng, M["PT_copied_dve" if j % 2 else "PT_copied_act"], t * (SLOTS // 2) + j // 2 + 1)

        NA = 8
        NC = 6
        NF = (5, 4)

        def xrow(ap, t, i):
            if isinstance(t, int):
                r0 = t * STEP + i * P
                return ap[r0:r0 + P, :]
            return ap[bass.ds(t * STEP + i * P, P), :]

        block = ctx.enter_context(nc.Block())

        @block.sync
        def _(sp):
            def load_x(t, i):
                need(sp, M["a_xn"], (t - 1) * TILES + i + 1)
                sp.dma_start(xa[:, i, :], xrow(A["x"], t, i)).then_inc(M[f"xa_in{i}"], 16)

            def stack(t, p, hg):
                ring = 1 + p % (RING // STEP)
                sp.wait_ge(M["qk_hi_done"], t * NGROUP + hg + 1)
                sp.wait_ge(M["qk_lo_done"], t * NGROUP + hg + 1)
                for r in range(GROUP):
                    parts = qkp[r * HD:(r + 1) * HD, hg % 2].rearrange("p w a n -> p (w a) n")
                    for term, (qpart, kpart) in enumerate(((0, 0), (0, 1), (1, 0))):
                        kplace = 2 + kpart
                        sp.dma_start(QK3[term * HD:(term + 1) * HD, hg * GROUP + r, 0:ring + 1:ring],
                                     parts[:, qpart:kplace + 1:kplace - qpart]).then_inc(M[f"stacked{hg}"], 16)

            def body(it):
                for s in range(SLOTS):
                    for t, p, _ in due(it, X_SLOT, s, 0, 2):
                        for i in range(TILES):
                            load_x(t, i)
                    for t, p, (hg, w) in due(it, QK_SLOT, s, 2, 1):
                        if w == 1:
                            stack(t, p, hg)
                    for t, p, (i, piece) in due(it, FF2_SLOT, s, 3, -1):
                        if piece == FF2_PIECES - 1:
                            sp.wait_ge(M["c_out"], t * TILES + i + 1)
                            sp.dma_start(xrow(out, t, i), yc[:, i, :]).then_inc(M[f"stored{i}"], 16)
                    for t, p, i in due(it, XR_SLOT, s, 0, -1):
                        need(sp, M["c_out"], (t - 1) * TILES + i + 1)
                        sp.dma_start(x1[:, i, :], xrow(A["x"], t, i)).then_inc(M[f"xr_in{i}"], 16)

            for i in range(TILES):
                load_x(0, i)
            run_iterations(sp, body)
            for i in range(TILES):
                sp.wait_ge(M[f"stored{i}"], 16 * NSTEP)

        @block.tensor
        def _(pe):
            def scores(t, p, j):
                hg, qc, r = block_of(j)
                h = hg * GROUP + r
                if qc == 0 and r == 0:
                    pe.wait_ge(M[f"stacked{hg}"], (t + 1) * 3 * GROUP * 16)
                need(pe, M["S_done"], t * SLOTS + j - 1)
                kc = key_chunks(p, qc)
                runs = []
                for place, c in kc:
                    if runs and (c % (RING // P)) == runs[-1][1] + runs[-1][2]:
                        runs[-1][2] += 1
                    else:
                        runs.append([place, c % (RING // P), 1])
                for place, slot, n in runs:
                    mm = pe.matmul(Sb[j % 2][:, place * P:(place + n) * P], Q3[:, h, qc * P:(qc + 1) * P],
                                   K3[:, h, slot * P:(slot + n) * P], start=True, stop=True,
                                   skip_group_check=True)
                mm.then_inc(M["S_full"], 1)

            def transposes(t, p, j):
                hg, qc, r = block_of(j)
                pe.wait_ge(M["S_exp"], t * SLOTS + j + 1)
                copied(pe, t, j - 1)
                for place, _ in key_chunks(p, qc):
                    mm = pe.transpose(PTb[:, place * P:(place + 1) * P],
                                      Sm[:, j % NSM, place * P:(place + 1) * P], W["idf"][:])
                mm.then_inc(M["T_full"], 1)

            def weighted_values(t, p, g):
                hg, qc = g // TILES, g % TILES
                copied(pe, t, GROUP * g + GROUP - 1)
                copied(pe, t, GROUP * g + GROUP - 2)
                if qc == 0:
                    need(pe, M["o32_done"], t * NGROUP + hg)
                pe.wait_ge(M["A_free"], t * NA + 2 + qc + 1)
                kc = key_chunks(p, qc)
                for n, (place, c) in enumerate(kc):
                    for r in range(GROUP):
                        j = g * GROUP + r
                        mm = pe.matmul(Ob[r * HD:(r + 1) * HD, qc * P:(qc + 1) * P],
                                       V[:, c, (hg * GROUP + r) * HD:(hg * GROUP + r + 1) * HD],
                                       PTs[:, j % NPT, place * P:(place + 1) * P],
                                       start=(n == 0), stop=(n == len(kc) - 1), skip_group_check=True)
                mm.then_inc(M["PT_used"], 1)

            def reciprocal_rows(t, hg):
                pe.wait_ge(M["rb_done"], t * NGROUP + hg + 1)
                for qc in range(TILES):
                    mm = pe.transpose(Ob[:, STEP + qc * P:STEP + (qc + 1) * P],
                                      rb[:, qc * GROUP:(qc + 1) * GROUP].rearrange("p r d -> p (r d)"),
                                      W["idf"][:])
                mm.then_inc(M["O_full"], 1)

            def product3(outp, a, b):
                n = 0
                for pa, pb in ((0, 0), (0, 1), (1, 0)):
                    for k in range(KD):
                        mm = pe.matmul(outp, a(pa, k), b(pb, k), start=(n == 0), stop=(n == 3 * KD - 1),
                                       skip_group_check=True)
                        n += 1
                return mm

            def a_transposes(t, i):
                need(pe, M["A_free"], t * NA + i)
                pe.wait_ge(M["a_xn"], t * TILES + i + 1)
                for k in range(KD):
                    mm = pe.transpose(Ab[:, k * P:(k + 1) * P], xn[:, i, k * P:(k + 1) * P], W["idf"][:])
                mm.then_inc(M["A_full"], 1)

            def values(t, i, half):
                if half == 0:
                    need(pe, M["A_free"], t * NA + 2 + i)
                cols = slice(half * D // 2, (half + 1) * D // 2)
                mm = product3(Ab[:, cols], lambda a, k: xT[:, a, k, i * P:(i + 1) * P],
                              lambda a, k: W["w"][:, 2, a, k, cols])
                if half == 1:
                    mm.then_inc(M["A_full"], 1)

            def queries_keys(t, hg, w):
                if w == 0:
                    need(pe, M["A_free"], t * NA + 4 + hg)
                mm = product3(Ab[:, w * STEP:(w + 1) * STEP],
                              lambda a, k: W["w"][:, w, a, k, hg * P:(hg + 1) * P],
                              lambda a, k: xT[:, a, k, :])
                if w == 1:
                    mm.then_inc(M["A_full"], 1)

            def out_projection(t, i, half):
                if half == 0:
                    need(pe, M["C_free"], t * (NC - 1) + i)
                pe.wait_ge(M["OT_hi"], (t + 1) * NGROUP)
                pe.wait_ge(M["OT_lo"], (t + 1) * NGROUP)
                cols = slice(half * D // 2, (half + 1) * D // 2)
                mm = product3(Cb[:, cols], lambda a, k: OT[:, a, k, i * P:(i + 1) * P],
                              lambda a, k: W["w"][:, 3, a, k, cols])
                if half == 1:
                    mm.then_inc(M["C_full"], 1)

            def c_transposes(t, i):
                need(pe, M["C_free"], t * (NC - 1) + 2 + i)
                pe.wait_ge(M["b_xn"], t * TILES + i + 1)
                for k in range(KD):
                    mm = pe.transpose(Cb[:, k * P:(k + 1) * P], x2n[:, i, k * P:(k + 1) * P], W["idf"][:])
                mm.then_inc(M["C_full"], 1)

            def low_rank(t):
                pe.wait_ge(M["C_free"], t * (NC - 1) + 2 * TILES)
                mm = product3(Cb[0:LR, 0:STEP], lambda a, k: W["v"][:, a, k, :], lambda a, k: x2T[:, a, k, :])
                mm.then_inc(M["C_full"], 1)

            def hidden(t, m):
                b = m % 2
                need(pe, M[f"F_free{b}"], t * NF[b] + m // 2)
                for half in range(2):
                    mc = 2 * m + half
                    for k in range(KD):
                        for part in range(2):
                            pe.matmul(Fb[b][:, half * STEP:(half + 1) * STEP],
                                      W["t1"][:, k, mc * P:(mc + 1) * P], x2T[:, part, k, :],
                                      start=(half == 0 and k == 0 and part == 0), stop=False,
                                      skip_group_check=True)

            def hidden_low_rank(t, m):
                if m == 0:
                    pe.wait_ge(M["z_done"], t + 1)
                b = m % 2
                for half in range(2):
                    mc = 2 * m + half
                    mm = pe.matmul(Fb[b][:, half * STEP:(half + 1) * STEP], W["u"][:, mc * P:(mc + 1) * P],
                                   z6[:], start=False, stop=True, skip_group_check=True)
                mm.then_inc(M[f"F_full{b}"], 1)

            def ff_out(t, i, q):
                o = Fb[0] if i else Cb
                if q == 0 and i == 0:
                    pe.wait_ge(M["z_r1"], t + 1)
                if q == 0 and i == 1:
                    pe.wait_ge(M["F_free0"], t * NF[0] + 4)
                if i == 0:
                    pairs = t * (KH // 2) + (q + 1) * KH // 2 // FF2_PIECES
                    pe.wait_ge(M["r2_lo"], pairs)
                    pe.wait_ge(M["r2_hi"], pairs)
                for m in range(q * KH // FF2_PIECES, (q + 1) * KH // FF2_PIECES):
                    for part in range(2):
                        mm = pe.matmul(o[:, :], r2[:, part, m, i * P:(i + 1) * P], W["t2"][:, m, :],
                                       start=(m == 0 and part == 0), stop=(m == KH - 1 and part == 1),
                                       skip_group_check=True)
                if q == FF2_PIECES - 1:
                    mm.then_inc(M["F_full0" if i else "C_full"], 1)

            def body(it):
                for s in range(SLOTS):
                    if it.has(0):
                        scores(it.t, it.p, s)
                    ok, t, p, j = lagged(it, s, LAG_T)
                    if ok:
                        transposes(t, p, j)
                    for t, p, m in due(it, FF1_SLOT, s, 1, -1):
                        hidden_low_rank(t, m)
                    ok, t, p, j = lagged(it, s, LAG_PV)
                    if ok and j % GROUP == GROUP - 1:
                        weighted_values(t, p, j // GROUP)
                        if j // GROUP % TILES == TILES - 1:
                            reciprocal_rows(t, j // GROUP // TILES)
                    for t, p, i in due(it, XT_SLOT, s, 0, 1):
                        a_transposes(t, i)
                    for t, p, (i, half) in due(it, V_SLOT, s, 0, 1):
                        values(t, i, half)
                    for t, p, (hg, w) in due(it, QK_SLOT, s, 0, 1):
                        queries_keys(t, hg, w)
                    for t, p, (i, half) in due(it, WO_SLOT, s, 0, -1):
                        out_projection(t, i, half)
                    for t, p, i in due(it, X2_SLOT, s, 0, -1):
                        c_transposes(t, i)
                    for t, p, _ in due(it, Z_SLOT, s, 0, -1):
                        low_rank(t)
                    for t, p, m in due(it, FF1_SLOT, s, 0, -1):
                        hidden(t, m)
                    for t, p, (i, piece) in due(it, FF2_SLOT, s, 0, -1):
                        ff_out(t, i, piece)

            run_iterations(pe, body)

        @block.scalar
        def _(act):
            def exponentials(t, p, j):
                hg, qc, r = block_of(j)
                c0 = key_chunks(p, qc)[0][0] * P
                act.wait_ge(M["S_done"], t * SLOTS + j + 1)
                blk = Sm[:, j % NSM, c0:WIN]
                act.activation(blk, blk, ACT.Exp, bias=nmax[:, j % 8:j % 8 + 1], scale=-1.0,
                               accum_out=sums[:, hg % 2, qc, r:r + 1]).then_inc(M["S_exp"], 1)

            def copy_transposed(t, p, j):
                c0 = key_chunks(p, block_of(j)[1])[0][0] * P
                act.wait_ge(M["T_full"], t * SLOTS + j + 1)
                need(act, M["PT_used"], t * (SLOTS // GROUP) + (j - NPT) // GROUP + 1)
                act.activation(PTs[:, j % NPT, c0:WIN], PTb[:, c0:WIN], ACT.Copy).then_inc(M["PT_copied_act"], 1)

            def sum_rows(t, hg):
                act.wait_ge(M["O_full"], t * NGROUP + hg + 1)
                need(act, M["o32_done"], t * NGROUP + hg)
                act.activation(Rs[:], Ob[:, STEP:2 * STEP], ACT.Copy).then_inc(M["Rs_done"], 1)

            def out_hi(t, hg):
                act.wait_ge(M["o32_done"], t * NGROUP + hg + 1)
                need(act, M["C_full"], (t - 1) * NC + 2)
                act.activation(OT[:, 0, hg, :], o32[:], ACT.Copy).then_inc(M["OT_hi"], 1)

            def a_hi(t, i):
                act.wait_ge(M["A_full"], t * NA + i + 1)
                act.activation(xT[:, 0, :, i * P:(i + 1) * P], Ab[:, :].rearrange("p (k n) -> p k n", k=KD),
                               ACT.Copy).then_inc(M["a_xh"], 1)

            def qk_bias(t, hg):
                act.wait_ge(M["A_full"], t * NA + 4 + hg + 1)
                need(act, M["qk_hi_done"], t * NGROUP + hg - 1)
                need(act, M["qk_lo_done"], t * NGROUP + hg - 1)
                act.activation(qk32[:, hg % 2, 0], Ab[:, 0:STEP], ACT.Identity, bias=W["bqs"][:, 0, hg:hg + 1],
                               scale=W["c"][:, 0:1])
                act.activation(qk32[:, hg % 2, 1], Ab[:, STEP:2 * STEP], ACT.Identity,
                               bias=W["bqs"][:, 1, hg:hg + 1], scale=W["c"][:, 1:2]).then_inc(M["A_free"], 1)

            def b_hi(t, i):
                act.wait_ge(M["C_full"], t * NC + 2 + i + 1)
                need(act, M["F_full1"], t * NF[1])
                act.activation(x2T[:, 0, :, i * P:(i + 1) * P], Cb[:, :].rearrange("p (k n) -> p k n", k=KD),
                               ACT.Copy).then_inc(M["b_xh"], 1)

            def z_first(t):
                act.wait_ge(M["C_full"], t * NC + 5)
                act.activation(z_h[:], Cb[0:LR, 0:STEP], ACT.Copy).then_inc(M["z_hi"], 1)

            def z_second(t):
                act.wait_ge(M["z_r1"], t + 1)
                act.activation(z_m[:], z_r[:], ACT.Copy).then_inc(M["z_mid"], 1)

            def relu_square(t, m):
                b = m % 2
                act.wait_ge(M[f"F_full{b}"], t * NF[b] + m // 2 + 1)
                need(act, M["r2_sq"], t * (KH // 2) + m - 1)
                need(act, M["r2_hi"], t * (KH // 2) + m - 1)
                for half in range(2):
                    ins = act.activation(r32[:, b, half * STEP:(half + 1) * STEP],
                                         Fb[b][:, half * STEP:(half + 1) * STEP], ACT.Relu,
                                         scale=W["c1"][:, 2 * m + half:2 * m + half + 1])
                ins.then_inc(M[f"F_free{b}"], 1)
                act.wait_ge(M[f"F_free{b}"], t * NF[b] + m // 2 + 1)
                need(act, M["F_full0"], t * NF[0])
                act.activation(r2[:, 0, 2 * m:2 * m + 2, :].rearrange("p m n -> p (m n)"), r32[:, m % 2],
                               ACT.Square).then_inc(M["r2_hi"], 1)

            def body(it):
                for s in range(SLOTS):
                    for t, p, i in due(it, XT_SLOT, s, 1, 1):
                        a_hi(t, i)
                    for t, p, i in due(it, X2_SLOT, s, 1, -1):
                        b_hi(t, i)
                    if it.has(0):
                        exponentials(it.t, it.p, s)
                    ok, t, p, j = lagged(it, s, LAG_O)
                    if ok and j % (TILES * GROUP) == TILES * GROUP - 1:
                        sum_rows(t, block_of(j)[0])
                    ok, t, p, j = lagged(it, s, LAG_T)
                    if ok and j % 2 == 0:
                        copy_transposed(t, p, j)
                    ok, t, p, j = lagged(it, s, LAG_OT)
                    if ok and j % (TILES * GROUP) == TILES * GROUP - 1:
                        out_hi(t, block_of(j)[0])
                    for t, p, (hg, w) in due(it, QK_SLOT, s, 1, 1):
                        if w == 1:
                            qk_bias(t, hg)
                    for t, p, _ in due(it, Z_SLOT, s, 0, -1):
                        z_first(t)
                    for t, p, _ in due(it, Z_SLOT, s, 1, -1):
                        z_second(t)
                    for t, p, m in due(it, FF1_SLOT, s, 1, -1):
                        relu_square(t, m)

            run_iterations(act, body)

        @block.vector
        def _(v):
            def masked_scores(t, p, j):
                hg, qc, r = block_of(j)
                c0 = key_chunks(p, qc)[0][0] * P
                need(v, M["T_full"], t * SLOTS + j - NSM + 1)
                settled_wait(v, W["consts"], M["S_full"], t * SLOTS + j + 1)
                v.tensor_tensor_reduce(Sm[:, j % NSM, c0:WIN], Sb[j % 2][:, c0:WIN], W["mask"][:, c0:WIN],
                                       W["c"][:, 3:4], 3e38, ALU.add, ALU.min,
                                       nmax[:, j % 8:j % 8 + 1]).then_inc(M["S_done"], 1)

            def copy_transposed(t, p, j):
                c0 = key_chunks(p, block_of(j)[1])[0][0] * P
                v.wait_ge(M["T_full"], t * SLOTS + j + 1)
                need(v, M["PT_used"], t * (SLOTS // GROUP) + (j - NPT) // GROUP + 1)
                v.tensor_copy(PTs[:, j % NPT, c0:WIN], PTb[:, c0:WIN]).then_inc(M["PT_copied_dve"], 1)

            def reciprocals(t, hg):
                v.wait_ge(M["S_exp"], t * SLOTS + (hg + 1) * TILES * GROUP)
                need(v, M["rb_done"], t * NGROUP + hg)
                v.reciprocal(rinv[:].rearrange("p a o -> p (a o)"),
                             sums[:, hg % 2].rearrange("p a r -> p (a r)")).then_inc(M["rinv_done"], 1)
                v.wait_ge(M["rinv_done"], t * NGROUP + hg + 1)
                need(v, M["O_full"], t * NGROUP + hg)
                v.tensor_copy(rb[:], rinv[:].to_broadcast([P, TILES * GROUP, HD])).then_inc(M["rb_done"], 1)

            def normalised(t, hg):
                v.wait_ge(M["Rs_done"], t * NGROUP + hg + 1)
                need(v, M["OT_hi"], t * NGROUP + hg)
                need(v, M["OT_lo"], t * NGROUP + hg)
                v.tensor_tensor(o32[:], Ob[:, 0:STEP], Rs[:], ALU.mult).then_inc(M["o32_done"], 1)

            def ln_stats(k, row, x, n):
                v.bn_stats(lnst[:, row, :], x).then_inc(M[k + "_st"], 1)
                settled_wait(v, W["consts"], M[k + "_st"], n + 1)
                v.bn_aggr(lnmv[:, row, :], lnst[:, row, :]).then_inc(M[k + "_mv"], 1)
                v.wait_ge(M[k + "_mv"], n + 1)

            def a_stats(t, i):
                n = t * TILES + i
                v.wait_ge(M[f"xa_in{i}"], (t + 1) * 16)
                ln_stats("a", 0, xa[:, i, :], n)
                v.tensor_scalar(lnve[:, 0, :], lnmv[:, 0, 1:2], EPS, XS ** -2, ALU.add,
                                ALU.mult).then_inc(M["a_ve"], 1)

            def a_norm(t, i):
                n = t * TILES + i
                v.wait_ge(M["a_rs"], n + 1)
                need(v, M["A_full"], (t - 1) * NA + i + 1)
                v.tensor_scalar(xn[:, i], xa[:, i, :], lnmv[:, 0, 0:1], lnrs[:, 0, 0:1], ALU.subtract,
                                ALU.mult).then_inc(M["a_xn"], 1)

            def a_lo(t, i):
                v.wait_ge(M["a_xh"], t * TILES + i + 1)
                v.tensor_tensor(xT[:, 1, :, i * P:(i + 1) * P], Ab[:, :].rearrange("p (k n) -> p k n", k=KD),
                                xT[:, 0, :, i * P:(i + 1) * P], ALU.subtract).then_inc(M["A_free"], 1)

            def v_evacuate(t, p, i):
                v.wait_ge(M["A_full"], t * NA + 2 + i + 1)
                need(v, M["PT_used"], (t - 2) * (SLOTS // GROUP))
                v.scalar_tensor_tensor(V[:, p * TILES + i, :], Ab[:, :], W["c"][:, 2:3], W["bv"][:],
                                       ALU.mult, ALU.add).then_inc(M["A_free"], 1)

            def qk_hi(t, hg):
                v.wait_ge(M["A_free"], t * NA + 4 + hg + 1)
                b, c = (hg - 2, t + 1) if hg >= 2 else (hg - 2 + NGROUP, t)
                need(v, M[f"stacked{b}"], c * 3 * GROUP * 16)
                v.tensor_copy(qkp[:, hg % 2, :, 0], qk32[:, hg % 2]).then_inc(M["qk_hi_done"], 1)

            def y_evacuate(t, i):
                n = t * TILES + i
                v.wait_ge(M["C_full"], t * NC + i + 1)
                need(v, M["x1_done"], (t - 1) * TILES + i + 1)
                v.scalar_tensor_tensor(yb[:, i], Cb[:, :], W["c"][:, 4:5], W["bo"][:], ALU.mult,
                                       ALU.add).then_inc(M["C_free"], 1)
                v.wait_ge(M["C_free"], t * (NC - 1) + i + 1)
                ln_stats("y", 1, yb[:, i], n)
                v.tensor_scalar(lnve[:, 1, :], lnmv[:, 1, 1:2], EPS, None, ALU.add).then_inc(M["y_ve"], 1)

            def y_norm(t, i):
                n = t * TILES + i
                v.wait_ge(M["y_rs"], n + 1)
                v.tensor_scalar(yb[:, i], yb[:, i], lnmv[:, 1, 0:1], lnrs[:, 1, 0:1], ALU.subtract,
                                ALU.mult).then_inc(M["y_n"], 1)

            def b_stats(t, i):
                n = t * TILES + i
                v.wait_ge(M["x1_done"], n + 1)
                ln_stats("b", 2, x1[:, i, :], n)
                v.tensor_scalar(lnve[:, 2, :], lnmv[:, 2, 1:2], EPS, XS ** -2, ALU.add,
                                ALU.mult).then_inc(M["b_ve"], 1)

            def b_norm(t, i):
                n = t * TILES + i
                v.wait_ge(M["b_rs"], n + 1)
                need(v, M["C_full"], (t - 1) * NC + TILES + i + 1)
                v.tensor_scalar(x2n[:, i], x1[:, i, :], lnmv[:, 2, 0:1], lnrs[:, 2, 0:1], ALU.subtract,
                                ALU.mult).then_inc(M["b_xn"], 1)

            def b_lo(t, i):
                v.wait_ge(M["b_xh"], t * TILES + i + 1)
                v.tensor_tensor(x2T[:, 1, :, i * P:(i + 1) * P], Cb[:, :].rearrange("p (k n) -> p k n", k=KD),
                                x2T[:, 0, :, i * P:(i + 1) * P], ALU.subtract).then_inc(M["C_free"], 1)

            def z_rest(t):
                v.wait_ge(M["z_hi"], t + 1)
                need(v, M["z_done"], t)
                v.scalar_tensor_tensor(z_r[:], z_h[:], W["zsel"][0:LR, 0:1], Cb[0:LR, 0:STEP], ALU.mult,
                                       ALU.add).then_inc(M["z_r1"], 1)

            def z_last(t):
                v.wait_ge(M["z_mid"], t + 1)
                need(v, M["F_full1"], t * NF[1])
                v.scalar_tensor_tensor(z6[:], z_m[:], W["zsel"][0:LR, 1:2], z_r[:], ALU.mult,
                                       ALU.add).then_inc(M["z_done"], 1)

            def square_lo(t, m):
                v.wait_ge(M["r2_sq"], t * (KH // 2) + m + 1)
                v.wait_ge(M["r2_hi"], t * (KH // 2) + m + 1)
                v.tensor_tensor(r2[:, 1, 2 * m:2 * m + 2, :].rearrange("p m n -> p (m n)"), sq32[:],
                                r2[:, 0, 2 * m:2 * m + 2, :].rearrange("p m n -> p (m n)"),
                                ALU.subtract).then_inc(M["r2_lo"], 1)

            def c_evacuate(t, i):
                n = t * TILES + i
                full, free, b = ("F_full0", "F_free0", Fb[0]) if i else ("C_full", "C_free", Cb)
                v.wait_ge(M[full], (t + 1) * (NF[0] if i else NC))
                if i == 0:
                    for k in range(TILES):
                        need(v, M[f"stored{k}"], t * 16)
                v.tensor_tensor(yc[:, i, :], b[:, :], W["s2"][:], ALU.mult).then_inc(M[free], 1)
                v.wait_ge(M[free], (t + 1) * (NF[0] if i else NC - 1))
                ln_stats("c", 3, yc[:, i, :], n)
                v.tensor_scalar(lnve[:, 3, :], lnmv[:, 3, 1:2], EPS, None, ALU.add).then_inc(M["c_ve"], 1)

            def c_norm(t, i):
                n = t * TILES + i
                v.wait_ge(M["c_rs"], n + 1)
                v.tensor_scalar(yc[:, i, :], yc[:, i, :], lnmv[:, 3, 0:1], lnrs[:, 3, 0:1], ALU.subtract,
                                ALU.mult).then_inc(M["c_n"], 1)

            def body(it):
                for s in range(SLOTS):
                    if it.has(0):
                        masked_scores(it.t, it.p, s)
                    for t, p, (i, half) in due(it, V_SLOT, s, 1, 1):
                        if half == 1:
                            v_evacuate(t, p, i)
                    ok, t, p, j = lagged(it, s, LAG_T)
                    if ok and j % 2:
                        copy_transposed(t, p, j)
                    ok, t, p, j = lagged(it, s, LAG_RB)
                    if ok and j % (TILES * GROUP) == TILES * GROUP - 1:
                        reciprocals(t, block_of(j)[0])
                    ok, t, p, j = lagged(it, s, LAG_O)
                    if ok and j % (TILES * GROUP) == TILES * GROUP - 1:
                        normalised(t, block_of(j)[0])
                    for t, p, i in due(it, A_STATS, s, 0, 1):
                        a_stats(t, i)
                    for t, p, i in due(it, A_NORM, s, 0, 1):
                        a_norm(t, i)
                    for t, p, i in due(it, XT_SLOT, s, 1, 1):
                        a_lo(t, i)
                    for t, p, (hg, w) in due(it, QK_SLOT, s, 2, 1):
                        if w == 1:
                            qk_hi(t, hg)
                    for t, p, (i, half) in due(it, WO_SLOT, s, 1, -1):
                        if half == 1:
                            y_evacuate(t, i)
                    for t, p, i in due(it, Y_NORM, s, 0, -1):
                        y_norm(t, i)
                    for t, p, i in due(it, B_STATS, s, 0, -1):
                        b_stats(t, i)
                    for t, p, i in due(it, B_NORM, s, 0, -1):
                        b_norm(t, i)
                    for t, p, i in due(it, X2_SLOT, s, 1, -1):
                        b_lo(t, i)
                    for t, p, _ in due(it, Z_SLOT, s, 1, -1):
                        z_rest(t)
                    for t, p, _ in due(it, Z_SLOT, s, 2, -1):
                        z_last(t)
                    for t, p, m in due(it, FF1_SLOT, s, 2, -1):
                        square_lo(t, m)
                    for t, p, (i, piece) in due(it, FF2_SLOT, s, 1, -1):
                        if piece == FF2_PIECES - 1:
                            c_evacuate(t, i)
                    for t, p, (i, piece) in due(it, FF2_SLOT, s, 2, -1):
                        if piece == FF2_PIECES - 1:
                            c_norm(t, i)

            run_iterations(v, body)

        @block.gpsimd
        def _(g):
            def rstd(k, row, n):
                g.wait_ge(M[k + "_ve"], n + 1)
                g.tensor_tensor(lnrs[:, row, 0:1], lnve[:, row, :], W["nhalf"][:], ALU.pow).then_inc(M[k + "_rs"], 1)

            def qk_lo(t, hg):
                g.wait_ge(M["qk_hi_done"], t * NGROUP + hg + 1)
                need(g, M["S_full"], (t - 1) * SLOTS + (hg + 1) * TILES * GROUP)
                g.tensor_tensor(qkp[:, hg % 2, :, 1], qk32[:, hg % 2], qkp[:, hg % 2, :, 0],
                                ALU.subtract).then_inc(M["qk_lo_done"], 1)

            def out_lo(t, hg):
                g.wait_ge(M["OT_hi"], t * NGROUP + hg + 1)
                g.tensor_tensor(OT[:, 1, hg, :], o32[:], OT[:, 0, hg, :], ALU.subtract).then_inc(M["OT_lo"], 1)

            def first_residual(t, i):
                n = t * TILES + i
                g.wait_ge(M["y_n"], n + 1)
                g.wait_ge(M[f"xr_in{i}"], (t + 1) * 16)
                g.tensor_tensor(x1[:, i, :], yb[:, i], x1[:, i, :], ALU.add).then_inc(M["x1_done"], 1)

            def square(t, m):
                g.wait_ge(M[f"F_free{m % 2}"], t * NF[m % 2] + m // 2 + 1)
                need(g, M["r2_lo"], t * (KH // 2) + m)
                g.tensor_tensor(sq32[:], r32[:, m % 2], r32[:, m % 2], ALU.mult).then_inc(M["r2_sq"], 1)

            def second_residual(t, i):
                n = t * TILES + i
                g.wait_ge(M["c_n"], n + 1)
                g.tensor_tensor(yc[:, i, :], yc[:, i, :], x1[:, i, :], ALU.add).then_inc(M["c_out"], 1)

            def body(it):
                for s in range(SLOTS):
                    for t, p, (hg, w) in due(it, QK_SLOT, s, 2, 1):
                        if w == 1:
                            qk_lo(t, hg)
                    ok, t, p, j = lagged(it, s, LAG_OT)
                    if ok and j % (TILES * GROUP) == TILES * GROUP - 1:
                        out_lo(t, block_of(j)[0])
                    for t, p, i in due(it, A_STATS, s, 0, 1):
                        rstd("a", 0, t * TILES + i)
                    for t, p, (i, half) in due(it, WO_SLOT, s, 1, -1):
                        if half == 1:
                            rstd("y", 1, t * TILES + i)
                    for t, p, i in due(it, Y_NORM, s, 0, -1):
                        first_residual(t, i)
                    for t, p, i in due(it, B_STATS, s, 0, -1):
                        rstd("b", 2, t * TILES + i)
                    for t, p, m in due(it, FF1_SLOT, s, 1, -1):
                        square(t, m)
                    for t, p, (i, piece) in due(it, FF2_SLOT, s, 1, -1):
                        if piece == FF2_PIECES - 1:
                            rstd("c", 3, t * TILES + i)
                    for t, p, (i, piece) in due(it, FF2_SLOT, s, 2, -1):
                        if piece == FF2_PIECES - 1:
                            second_residual(t, i)

            run_iterations(g, body)


def build(nc, A, out):
    with ExitStack() as ctx:
        def sb(name, shape, dt):
            return ctx.enter_context(nc.sbuf_tensor(name, shape, dt))

        W = {
            "w": sb("w_attn", [P, 4, 2, KD, D], F16),
            "t1": sb("t1", [P, KD, HIDDEN], F16),
            "t2": sb("t2", [P, KH, D], F16),
            "u": sb("u_T", [LR, HIDDEN], BF16),
            "v": sb("v_T", [P, 2, KD, LR], F16),
            "bo": sb("bo_rows", [P, D], F32), "bv": sb("bv_rows", [P, D], F32),
            "s2": sb("s2_rows", [P, D], F32),
            "mask": sb("mask", [P, WIN], F32),
            "idf": sb("idf", [P, P], F32), "idh": sb("idh", [P, P], F16),
            "nhalf": sb("nhalf", [P, 1], F32), "zsel": sb("zsel", [P, 2], F32),
            "c": sb("scales", [P, 12], F32), "c1": sb("c1", [P, KH], F32),
            "bqs": sb("bqs", [P, 2, KD], F32),
            "consts": ctx.enter_context(nc.semaphore("consts_ready")),
        }
        prepare(nc, A, W)
        steps(nc, A, W, out)


def kernel(**inputs):
    import numpy as np
    import concourse.bacc as bacc
    from concourse.bass_utils import run_bass_kernel_spmd

    nc = bacc.Bacc("TRN2", target_bir_lowering=False, num_devices=1)
    arrays, A = {}, {}
    for name, a in inputs.items():
        short = name.replace("L0_attn_", "").replace("L0_ffn_", "")
        a = np.ascontiguousarray(a)
        if short == "x":
            a = a.reshape(BATCH * SEQ, D)
        if short == "gate":
            a = a.reshape(1)
        arrays[f"in_{short}"] = a
        A[short] = nc.dram_tensor(f"in_{short}", a.shape, mybir.dt.from_np(a.dtype), kind="ExternalInput").ap()
    out = nc.dram_tensor("out_0", (BATCH * SEQ, D), F32, kind="ExternalOutput").ap()
    build(nc, A, out)
    r = run_bass_kernel_spmd(nc, [arrays], core_ids=[0])
    return r.results[0]["out_0"].reshape(BATCH, SEQ, D)
```
